# Optimizing a Trainium2 kernel written in Bass

```python
import numpy as np
import jax
import jax.numpy as jnp

def _softmax(x, axis=-1):
    return jax.nn.softmax(x, axis=axis)

def _gelu(x):
    return jax.nn.gelu(x, approximate=True)

def _silu(x):
    return jax.nn.silu(x)

def _sigmoid(x):
    return jax.nn.sigmoid(x)

def _layernorm(x, axis=-1, eps=1e-05):
    m = jnp.mean(x, axis=axis, keepdims=True)
    v = jnp.var(x, axis=axis, keepdims=True)
    return (x - m) / jnp.sqrt(v + eps)

def _scatter_add(tgt, idx, src, axis=0):
    return tgt.at[idx].add(src)

def _segment_sum(src, seg, n):
    return jax.ops.segment_sum(src, seg, n)
kernel_name = 'mk_macaron_d2_jaxref_r8_ff0330'

def setup_inputs(seed: int=0):
    np.random.seed(seed)
    _w = jnp.asarray

    def _L0_attn_setup():
        import jax, jax.numpy as jnp
        import numpy as np
        NUM_HEADS = 16
        NUM_LANDMARKS = 64
        DIM = 128
        B, N = (2, 1024)

        def iterative_inv(K, n_iter=6):
            m = K.shape[-1]
            I = jnp.eye(m, dtype=K.dtype)
            denom = jnp.max(jnp.sum(K, axis=-2), axis=-1)[..., None, None]
            V = jnp.swapaxes(K, -1, -2) / denom
            for _ in range(n_iter):
                KV = K @ V
                V = 0.25 * V @ (13.0 * I - KV @ (15.0 * I - KV @ (7.0 * I - KV)))
            return V

        def _reference_tuple_inner(x, w_qkv, w_proj):
            Bb, Nn, C = x.shape
            H = NUM_HEADS
            hd = C // H
            m = NUM_LANDMARKS
            scale = hd ** 0.5
            qkv = (x @ w_qkv).reshape(Bb, Nn, 3, H, hd).transpose(2, 0, 3, 1, 4)
            q, k, v = (qkv[0], qkv[1], qkv[2])
            q = q / scale
            k_lm = k.reshape(Bb, H, m, Nn // m, hd).mean(axis=-2)
            q_lm = q.reshape(Bb, H, m, Nn // m, hd).mean(axis=-2)
            kernel1 = jax.nn.softmax(jnp.einsum('bhnd,bhmd->bhnm', q, k_lm), axis=-1)
            kernel2 = jax.nn.softmax(jnp.einsum('bhld,bhmd->bhlm', q_lm, k_lm), axis=-1)
            kernel3 = jax.nn.softmax(jnp.einsum('bhmd,bhnd->bhmn', q_lm, k), axis=-1)
            SV = kernel1 @ iterative_inv(kernel2) @ (kernel3 @ v)
            SV = SV.transpose(0, 2, 1, 3).reshape(Bb, Nn, C)
            out = SV @ w_proj
            return (out, SV)
        key = jax.random.key(seed)
        k1, k2, k3 = jax.random.split(key, 3)
        x = jax.random.normal(k1, (B, N, DIM), dtype=jnp.float32)
        w_qkv = jax.random.normal(k2, (DIM, 3 * DIM), dtype=jnp.float32) * DIM ** (-0.5)
        w_proj = jax.random.normal(k3, (DIM, DIM), dtype=jnp.float32) * DIM ** (-0.5)
        return {'x': x, 'w_qkv': w_qkv, 'w_proj': w_proj}
    _L0_attn_in = _L0_attn_setup()

    def _L0_ffn_setup():
        import jax, jax.numpy as jnp
        import numpy as np
        import math
        GOLDEN_CENTER = 1.0 / math.e
        GOLDEN_LOWER = 0.5 - math.log(4.0 / 3.0)
        GOLDEN_UPPER = 0.5
        B, T, D = (4, 256, 128)
        E = 8
        I = 512 // (E // 2)

        def _routing_weights(x, Wr, temperature):
            inh = jax.nn.sigmoid(x @ Wr / temperature)
            in_zone = (inh >= GOLDEN_LOWER) & (inh <= GOLDEN_UPPER)
            dist = jnp.abs(inh - GOLDEN_CENTER)
            w = jnp.exp(-dist / 0.1) * in_zone.astype(x.dtype)
            wsum = w.sum(axis=-1, keepdims=True)
            no_expert = wsum < 1e-08
            fb = jnp.exp(-dist / 0.3)
            _, top2 = jax.lax.top_k(fb, 2)
            fb_mask = jax.nn.one_hot(top2, E, dtype=x.dtype).sum(axis=-2)
            fb_w = fb * fb_mask
            fb_w = fb_w / jnp.clip(fb_w.sum(axis=-1, keepdims=True), 1e-08)
            w = jnp.where(no_expert, fb_w, w)
            wsum = w.sum(axis=-1, keepdims=True)
            return w / jnp.clip(wsum, 1e-08)
        key = jax.random.key(seed)
        k = jax.random.split(key, 6)
        s_d = 1.0 / math.sqrt(D)
        s_i = 1.0 / math.sqrt(I)
        return {'x': jax.random.normal(k[0], (B, T, D), jnp.float32), 'Wg': jax.random.normal(k[1], (E, D, I), jnp.float32) * s_d, 'Wu': jax.random.normal(k[2], (E, D, I), jnp.float32) * s_d, 'Wd': jax.random.normal(k[3], (E, I, D), jnp.float32) * s_i, 'Wr': jax.random.normal(k[4], (D, E), jnp.float32) * s_d, 'temperature': jnp.ones((1,), jnp.float32)}
    _L0_ffn_in = _L0_ffn_setup()

    def _L1_attn_setup():
        import jax, jax.numpy as jnp
        import numpy as np
        D_MODEL = 128
        N_HEADS = 16
        HEAD_DIM = D_MODEL // N_HEADS
        WINDOW = 128

        def _window_starts(seq_len, window):
            starts = []
            for i in range(0, seq_len, window // 2):
                end = min(i + window, seq_len)
                starts.append(max(0, end - window))
                if end == seq_len:
                    break
            return np.asarray(starts, dtype=np.int32)
        key = jax.random.key(seed)
        ks = jax.random.split(key, 9)
        B, S = (4, 512)
        sc = 1.0 / np.sqrt(D_MODEL)
        return {'x': jax.random.normal(ks[0], (B, S, D_MODEL), jnp.float32), 'Wq': jax.random.normal(ks[1], (D_MODEL, D_MODEL), jnp.float32) * sc, 'bq': jax.random.normal(ks[2], (D_MODEL,), jnp.float32) * 0.02, 'Wk': jax.random.normal(ks[3], (D_MODEL, D_MODEL), jnp.float32) * sc, 'bk': jax.random.normal(ks[4], (D_MODEL,), jnp.float32) * 0.02, 'Wv': jax.random.normal(ks[5], (D_MODEL, D_MODEL), jnp.float32) * sc, 'bv': jax.random.normal(ks[6], (D_MODEL,), jnp.float32) * 0.02, 'Wo': jax.random.normal(ks[7], (D_MODEL, D_MODEL), jnp.float32) * sc, 'bo': jax.random.normal(ks[8], (D_MODEL,), jnp.float32) * 0.02}
    _L1_attn_in = _L1_attn_setup()

    def _L1_ffn_setup():
        import jax, jax.numpy as jnp
        import numpy as np
        TOPK = 4
        key = jax.random.key(seed)
        ks = jax.random.split(key, 9)
        B, T, D = (4, 256, 128)
        E, H = (32, 128)
        HS = H * TOPK
        s = lambda k, shape, fan: jax.random.normal(k, shape, dtype=jnp.float32) / np.sqrt(fan)
        return {'x': jax.random.normal(ks[0], (B, T, D), dtype=jnp.float32), 'router_w': s(ks[1], (E, D), D), 'router_bias': jnp.zeros((E,), dtype=jnp.float32), 'gate_w': s(ks[2], (E, H, D), D), 'up_w': s(ks[3], (E, H, D), D), 'down_w': s(ks[4], (E, D, H), H), 'sgate_w': s(ks[5], (HS, D), D), 'sup_w': s(ks[6], (HS, D), D), 'sdown_w': s(ks[7], (D, HS), HS)}
    _L1_ffn_in = _L1_ffn_setup()
    _d = {'L0_attn_x': _L0_attn_in['x'], 'L0_attn_w_qkv': _L0_attn_in['w_qkv'], 'L0_attn_w_proj': _L0_attn_in['w_proj'], 'L0_ffn_Wg': _L0_ffn_in['Wg'], 'L0_ffn_Wu': _L0_ffn_in['Wu'], 'L0_ffn_Wd': _L0_ffn_in['Wd'], 'L0_ffn_Wr': _L0_ffn_in['Wr'], 'L0_ffn_temperature': _L0_ffn_in['temperature'], 'L1_attn_Wq': _L1_attn_in['Wq'], 'L1_attn_bq': _L1_attn_in['bq'], 'L1_attn_Wk': _L1_attn_in['Wk'], 'L1_attn_bk': _L1_attn_in['bk'], 'L1_attn_Wv': _L1_attn_in['Wv'], 'L1_attn_bv': _L1_attn_in['bv'], 'L1_attn_Wo': _L1_attn_in['Wo'], 'L1_attn_bo': _L1_attn_in['bo'], 'L1_ffn_router_w': _L1_ffn_in['router_w'], 'L1_ffn_router_bias': _L1_ffn_in['router_bias'], 'L1_ffn_gate_w': _L1_ffn_in['gate_w'], 'L1_ffn_up_w': _L1_ffn_in['up_w'], 'L1_ffn_down_w': _L1_ffn_in['down_w'], 'L1_ffn_sgate_w': _L1_ffn_in['sgate_w'], 'L1_ffn_sup_w': _L1_ffn_in['sup_w'], 'L1_ffn_sdown_w': _L1_ffn_in['sdown_w']}
    _x0 = _d['L0_attn_x']
    _d['L0_attn_x'] = jax.random.normal(jax.random.fold_in(jax.random.key(seed), 1), (4, 512, 128), dtype=_x0.dtype)
    del _x0
    return _d

def reference(L0_attn_x, L0_attn_w_qkv, L0_attn_w_proj, L0_ffn_Wg, L0_ffn_Wu, L0_ffn_Wd, L0_ffn_Wr, L0_ffn_temperature, L1_attn_Wq, L1_attn_bq, L1_attn_Wk, L1_attn_bk, L1_attn_Wv, L1_attn_bv, L1_attn_Wo, L1_attn_bo, L1_ffn_router_w, L1_ffn_router_bias, L1_ffn_gate_w, L1_ffn_up_w, L1_ffn_down_w, L1_ffn_sgate_w, L1_ffn_sup_w, L1_ffn_sdown_w):

    def _L0_attn_ref(x, w_qkv, w_proj):
        import jax, jax.numpy as jnp
        import numpy as np
        NUM_HEADS = 16
        NUM_LANDMARKS = 64
        DIM = 128
        B, N = (2, 1024)

        def iterative_inv(K, n_iter=6):
            m = K.shape[-1]
            I = jnp.eye(m, dtype=K.dtype)
            denom = jnp.max(jnp.sum(K, axis=-2), axis=-1)[..., None, None]
            V = jnp.swapaxes(K, -1, -2) / denom
            for _ in range(n_iter):
                KV = K @ V
                V = 0.25 * V @ (13.0 * I - KV @ (15.0 * I - KV @ (7.0 * I - KV)))
            return V

        def _reference_tuple_inner(x, w_qkv, w_proj):
            Bb, Nn, C = x.shape
            H = NUM_HEADS
            hd = C // H
            m = NUM_LANDMARKS
            scale = hd ** 0.5
            qkv = (x @ w_qkv).reshape(Bb, Nn, 3, H, hd).transpose(2, 0, 3, 1, 4)
            q, k, v = (qkv[0], qkv[1], qkv[2])
            q = q / scale
            k_lm = k.reshape(Bb, H, m, Nn // m, hd).mean(axis=-2)
            q_lm = q.reshape(Bb, H, m, Nn // m, hd).mean(axis=-2)
            kernel1 = jax.nn.softmax(jnp.einsum('bhnd,bhmd->bhnm', q, k_lm), axis=-1)
            kernel2 = jax.nn.softmax(jnp.einsum('bhld,bhmd->bhlm', q_lm, k_lm), axis=-1)
            kernel3 = jax.nn.softmax(jnp.einsum('bhmd,bhnd->bhmn', q_lm, k), axis=-1)
            SV = kernel1 @ iterative_inv(kernel2) @ (kernel3 @ v)
            SV = SV.transpose(0, 2, 1, 3).reshape(Bb, Nn, C)
            out = SV @ w_proj
            return (out, SV)
        return _reference_tuple_inner(x, w_qkv, w_proj)[0]

    def _L0_ffn_ref(x, Wg, Wu, Wd, Wr, temperature):
        import jax, jax.numpy as jnp
        import numpy as np
        import math
        GOLDEN_CENTER = 1.0 / math.e
        GOLDEN_LOWER = 0.5 - math.log(4.0 / 3.0)
        GOLDEN_UPPER = 0.5
        B, T, D = (4, 256, 128)
        E = 8
        I = 512 // (E // 2)

        def _routing_weights(x, Wr, temperature):
            inh = jax.nn.sigmoid(x @ Wr / temperature)
            in_zone = (inh >= GOLDEN_LOWER) & (inh <= GOLDEN_UPPER)
            dist = jnp.abs(inh - GOLDEN_CENTER)
            w = jnp.exp(-dist / 0.1) * in_zone.astype(x.dtype)
            wsum = w.sum(axis=-1, keepdims=True)
            no_expert = wsum < 1e-08
            fb = jnp.exp(-dist / 0.3)
            _, top2 = jax.lax.top_k(fb, 2)
            fb_mask = jax.nn.one_hot(top2, E, dtype=x.dtype).sum(axis=-2)
            fb_w = fb * fb_mask
            fb_w = fb_w / jnp.clip(fb_w.sum(axis=-1, keepdims=True), 1e-08)
            w = jnp.where(no_expert, fb_w, w)
            wsum = w.sum(axis=-1, keepdims=True)
            return w / jnp.clip(wsum, 1e-08)
        weights = _routing_weights(x, Wr, temperature)
        gate = jnp.einsum('btd,edi->beti', x, Wg)
        up = jnp.einsum('btd,edi->beti', x, Wu)
        h = jax.nn.silu(gate) * up
        e_out = jnp.einsum('beti,eid->betd', h, Wd)
        out = jnp.einsum('bte,betd->btd', weights, e_out)
        return out

    def _L1_attn_ref(x, Wq, bq, Wk, bk, Wv, bv, Wo, bo):
        import jax, jax.numpy as jnp
        import numpy as np
        D_MODEL = 128
        N_HEADS = 16
        HEAD_DIM = D_MODEL // N_HEADS
        WINDOW = 128

        def _window_starts(seq_len, window):
            starts = []
            for i in range(0, seq_len, window // 2):
                end = min(i + window, seq_len)
                starts.append(max(0, end - window))
                if end == seq_len:
                    break
            return np.asarray(starts, dtype=np.int32)
        B, S, D = x.shape
        q = x @ Wq + bq
        k = x @ Wk + bk
        v = x @ Wv + bv
        starts = _window_starts(S, WINDOW)
        idx = starts[:, None] + np.arange(WINDOW)[None, :]
        idx_j = jnp.asarray(idx)
        qw = q[:, idx_j]
        kw = k[:, idx_j]
        vw = v[:, idx_j]
        scores = jnp.einsum('bwqd,bwkd->bwqk', qw, kw) / np.sqrt(HEAD_DIM)
        attn = jax.nn.softmax(scores, axis=-1)
        out_w = jnp.einsum('bwqk,bwkd->bwqd', attn, vw)
        flat_idx = idx.reshape(-1)
        out = jnp.zeros((B, S, D), x.dtype).at[:, flat_idx].add(out_w.reshape(B, -1, D))
        counts = jnp.zeros((S,), x.dtype).at[flat_idx].add(1.0)
        out = out / counts[None, :, None]
        return out @ Wo + bo

    def _L1_ffn_ref(x, router_w, router_bias, gate_w, up_w, down_w, sgate_w, sup_w, sdown_w):
        import jax, jax.numpy as jnp
        import numpy as np
        TOPK = 4
        B, T, D = x.shape
        flat = x.reshape(B * T, D)
        logits = flat.astype(jnp.float32) @ router_w.T + router_bias
        scores = jax.nn.softmax(logits, axis=-1)
        topk_scores, topk_idx = jax.lax.top_k(scores, TOPK)
        topk_scores = topk_scores / jnp.clip(topk_scores.sum(axis=-1, keepdims=True), 1e-12, None)
        h = jax.nn.silu(jnp.einsum('nd,ehd->neh', flat, gate_w)) * jnp.einsum('nd,ehd->neh', flat, up_w)
        expert_out = jnp.einsum('neh,edh->ned', h, down_w)
        sel = jnp.take_along_axis(expert_out, topk_idx[:, :, None], axis=1)
        out = (sel * topk_scores.astype(flat.dtype)[:, :, None]).sum(axis=1)
        out = out + jax.nn.silu(flat @ sgate_w.T) * (flat @ sup_w.T) @ sdown_w.T
        return out.reshape(B, T, D)
    x = L0_attn_x
    x = x + 0.5 * _L0_ffn_ref(_layernorm(x, axis=-1), L0_ffn_Wg, L0_ffn_Wu, L0_ffn_Wd, L0_ffn_Wr, L0_ffn_temperature)
    x = x + _L0_attn_ref(_layernorm(x, axis=-1), L0_attn_w_qkv, L0_attn_w_proj)
    x = x + 0.5 * _L0_ffn_ref(_layernorm(x, axis=-1), L0_ffn_Wg, L0_ffn_Wu, L0_ffn_Wd, L0_ffn_Wr, L0_ffn_temperature)
    x = x + 0.5 * _L1_ffn_ref(_layernorm(x, axis=-1), L1_ffn_router_w, L1_ffn_router_bias, L1_ffn_gate_w, L1_ffn_up_w, L1_ffn_down_w, L1_ffn_sgate_w, L1_ffn_sup_w, L1_ffn_sdown_w)
    x = x + _L1_attn_ref(_layernorm(x, axis=-1), L1_attn_Wq, L1_attn_bq, L1_attn_Wk, L1_attn_bk, L1_attn_Wv, L1_attn_bv, L1_attn_Wo, L1_attn_bo)
    x = x + 0.5 * _L1_ffn_ref(_layernorm(x, axis=-1), L1_ffn_router_w, L1_ffn_router_bias, L1_ffn_gate_w, L1_ffn_up_w, L1_ffn_down_w, L1_ffn_sgate_w, L1_ffn_sup_w, L1_ffn_sdown_w)
    return x

_drawn_inputs = setup_inputs


def setup_inputs(seed=0):
    import zlib

    import numpy as np

    out = dict(_drawn_inputs(seed))
    spreads = {'L1_ffn_router_bias': (0.0, 0.1)}
    factors = {'L1_attn_bq': 2.772, 'L1_attn_bk': 8.0, 'L1_attn_bo': 2.912}
    for name, (base, spread) in spreads.items():
        noise = np.random.default_rng([zlib.crc32(name.encode()), seed]).standard_normal(out[name].shape)
        drawn = base * np.exp(spread * noise) if base else spread * noise
        out[name] = jnp.asarray(drawn.astype(out[name].dtype))
    for name, factor in factors.items():
        out[name] = (out[name] * factor).astype(out[name].dtype)
    return out
```

```python
import math
from contextlib import ExitStack, contextmanager

import numpy as np
import concourse.bass as bass
from concourse import mybir

F32 = mybir.dt.float32
U32 = mybir.dt.uint32
ALU = mybir.AluOpType
ACT = mybir.ActivationFunctionType
AX = mybir.AxisListType.X
P = 128


class Track:

    def __init__(self, sem, step=1):
        self.sem, self.step = sem, step
        self.base, self.local, self.per_iter, self.i = 0, 0, None, None

    def now(self):
        if self.i is None:
            return self.sem, self.base + self.local
        return self.sem, self.i * self.per_iter + (self.base + self.local)

    def mark(self, instruction):
        instruction.then_inc(self.sem, self.step)
        self.local += self.step
        return self.now()


def need(engine, *values):
    for sem, value in values:
        if not (isinstance(value, int) and value <= 0):
            engine.wait_ge(sem, value)


@contextmanager
def loop(nc, count, marks):
    with nc.Fori(0, count) as i:
        for t, n in marks.items():
            t.base, t.local, t.per_iter, t.i = t.base + t.local, 0, n * t.step, i
        yield i
        wrong = {t.sem.name: t.local // t.step for t, n in marks.items() if t.local != n * t.step}
        assert not wrong, f"marks per iteration: {wrong}"
        for t in marks:
            t.base, t.local, t.i = t.base + count * t.per_iter, 0, None


def build(nc, a, out):
    B, S, D = a["x"].shape
    T = B * S
    NT = T // P
    TB = S // P
    GW = 4 * P
    NG = T // GW
    PE, DVE, SCL, POOL, SP = nc.tensor, nc.vector, nc.scalar, nc.gpsimd, nc.sync

    with ExitStack() as ctx:
        tracks = {}

        def sb(name, shape, dt=F32):
            return ctx.enter_context(nc.sbuf_tensor(name, shape, dt))

        def track(name, step=1):
            if name not in tracks:
                tracks[name] = Track(ctx.enter_context(nc.semaphore(name)), step)
            return tracks[name]

        for name in LOOP_TRACKS:
            t = track(name, 16 if "load" in name else 1)
            SP.sem_inc(t.sem, t.step)
            t.local = t.step
        nc.all_engine_barrier()

        bank = [ctx.enter_context(nc.psum_tensor(f"bank{n}", [P, 512], F32)) for n in range(8)]

        x = sb("x", [P, NT, D])
        xn = sb("xn", [P, NT, D])
        xnT = sb("xnT", [P, T])
        ident = sb("ident", [P, P])
        ident2 = sb("ident2", [P, 64])
        headmask = sb("headmask", [P, 16])
        blockones = sb("blockones", [P, P])
        iota_e = sb("iota_e", [P, 32])
        stats = sb("stats", [P, NT, 6])
        mv = sb("mv", [P, NT, 2])
        rstd = sb("rstd", [P, NT])

        s_x = track("x_loaded", 16)
        s_w = track("small_loaded", 16)
        s_c = track("const_pool")
        s_cv = track("const_dve")

        xr = a["x"].rearrange("b (t p) d -> p (b t) d", p=P)
        s_x.mark(SP.dma_start(x[:, :, :], xr))

        def load(name, shape, src):
            t = sb(name, shape)
            s_w.mark(SCL.dma_start(t[:], src))
            return t

        Wr0 = load("Wr0", [D, 8], a["Wr"])
        temp = load("temp", [P, 1], a["temp"].rearrange("(o a) -> o a", o=1).broadcast_to([P, 1]))
        wqkv = load("wqkv", [D, 3 * D], a["wqkv"])
        wproj = load("wproj", [D, D], a["wproj"])
        Wr1 = load("Wr1", [D, 32], a["WrT"])
        rbias = load("rbias", [P, 32], a["rbias"].rearrange("(o a) -> o a", o=1).broadcast_to([P, 32]))
        wq1, wk1, wv1, wo1 = (load(n, [D, D], a[n]) for n in ("Wq", "Wk", "Wv", "Wo"))
        bq1, bk1 = (load(n, [D, 1], a[n].rearrange("(d o) -> d o", o=1)) for n in ("bq", "bk"))
        bv1, bo1 = (load(n, [P, D], a[n].rearrange("(o d) -> o d", o=1).broadcast_to([P, D])) for n in ("bv", "bo"))

        s_c.mark(POOL.memset(ident[:, :], 0.0))
        s_c.mark(POOL.memset(ident2[:, :], 0.0))
        s_c.mark(POOL.memset(headmask[:, :], 1.0))
        s_c.mark(POOL.iota(iota_e[:, :], pattern=[[1, 32]], base=0, channel_multiplier=0,
                           allow_small_or_imprecise_dtypes=True))
        need(POOL, s_c.now())
        s_c.mark(POOL.affine_select(out=ident[:, :], in_=ident[:, :], compare_op=ALU.not_equal, fill=1.0,
                                    base=0, pattern=[[-1, P]], channel_multiplier=1))
        for base in (0, -64):
            s_c.mark(POOL.affine_select(out=ident2[:, :], in_=ident2[:, :], compare_op=ALU.not_equal, fill=1.0,
                                        base=base, pattern=[[-1, 64]], channel_multiplier=1))
            need(POOL, s_c.now())
        s_c.mark(POOL.affine_select(out=headmask[:, :], in_=headmask[:, :], compare_op=ALU.is_ge, fill=0.0,
                                    base=0, pattern=[[-8, 16]], channel_multiplier=1))
        need(POOL, s_c.now())
        s_c.mark(POOL.affine_select(out=headmask[:, :], in_=headmask[:, :], compare_op=ALU.is_ge, fill=0.0,
                                    base=7, pattern=[[8, 16]], channel_multiplier=-1))
        mhalf = sb("mhalf", [P, NT])
        s_c.mark(POOL.memset(mhalf[:, :], -0.5))
        s_cv.mark(DVE.memset(blockones[0:64, 0:64], 1.0))
        s_cv.mark(DVE.memset(blockones[0:64, 64:P], 0.0))
        s_cv.mark(DVE.memset(blockones[64:P, 0:64], 0.0))
        s_cv.mark(DVE.memset(blockones[64:P, 64:P], 1.0))
        need(DVE, s_w.now())
        s_cv.mark(DVE.reciprocal(temp[:, 0:1], temp[:, 0:1]))
        for e in (PE, SCL, DVE):
            need(e, s_c.now(), s_cv.now(), s_w.now(), s_x.now())
        need(POOL, s_cv.now(), s_w.now(), s_x.now())

        s_res = track("x_updated")

        rs_pow = track("rstd_pow")

        def inverse_std(n, tr):
            need(POOL, tr.mark(DVE.tensor_scalar(rstd[:, 0:n], mv[:, 0:n, 1], 1e-5, None, ALU.add)))
            need(DVE, rs_pow.mark(POOL.tensor_tensor(rstd[:, 0:n], rstd[:, 0:n], mhalf[:, 0:n], ALU.pow)))

        def layernorm_T():
            chain, norm, tr, ev = track("ln_chain"), track("ln_norm"), track("ln_transposed"), track("ln_evacuated")
            for e in (DVE, PE, SCL):
                need(e, s_res.now())
            for t in range(NT):
                chain.mark(DVE.bn_stats(out=stats[:, t, :], in_=x[:, t, :]))
            need(DVE, chain.now())
            for t in range(NT):
                chain.mark(DVE.bn_aggr(out=mv[:, t, :], in_=stats[:, t, :]))
            need(DVE, chain.now())
            inverse_std(NT, chain)
            for t in range(NT):
                norm.mark(DVE.tensor_scalar(xn[:, t, :], x[:, t, :], mv[:, t, 0:1], rstd[:, t:t + 1],
                                            ALU.subtract, ALU.mult))
                if t % 4 == 3:
                    b = bank[t // 4 % 2]
                    need(PE, norm.now())
                    if t // 4 >= 2:
                        need(PE, freed[t // 4 - 2])
                    else:
                        freed = [] if t == 3 else freed
                    for j in range(4):
                        tt = t - 3 + j
                        last = PE.transpose(b[:, j * P:(j + 1) * P], xn[:, tt, :], ident[:, :])
                    tr.mark(last)
                    need(SCL, tr.now())
                    freed.append(ev.mark(SCL.copy(xnT[:, (t - 3) * P:(t + 1) * P], b[:, :])))
            return ev.now()

        wbuf = [sb(f"wbuf{p}", [P, 3, P]) for p in range(2)]
        sg = [sb(f"sg{p}", [P, GW]) for p in range(2)]
        hT = [sb(f"hT{p}", [P, GW]) for p in range(2)]
        wtab = sb("wtab", [P, NT, 36])

        def expert_loop(E, weights, tag, ready):
            ld = [track(f"expert_load{p}", 16) for p in range(2)]
            gate, up, down = track("expert_gate"), track("expert_up"), track("expert_down")
            silu, hid, acc = track("expert_silu"), track("expert_hidden"), s_res
            psG, psU, psO = bank[0:2], bank[2:4], bank[4:6]

            def load(e, p):
                need(SP, down.now())
                ld[p].mark(SP.dma_start(wbuf[p][:, :, :], weights[bass.ds(e, 1), :, :, :]
                                        .rearrange("o p k n -> p (o k) n")))

            def gate_up(p, g, q, gate_free, up_free, hid_loaded):
                cols = slice(g * GW, (g + 1) * GW)
                need(PE, gate_free, hid_loaded)
                gate.mark(PE.matmul(psG[q][:, :], wbuf[p][:, 0, :], xnT[:, cols], start=True, stop=True))
                need(PE, up_free)
                up.mark(PE.matmul(psU[q][:, :], wbuf[p][:, 1, :], xnT[:, cols], start=True, stop=True))

            def finish(e, p, g, q, gate_at, up_at, sg_free, hT_free, acc_before):
                need(SCL, gate_at, sg_free)
                s = silu.mark(SCL.activation(sg[q][:, :], psG[q][:, :], ACT.Silu))
                need(DVE, s, up_at, hT_free)
                h = hid.mark(DVE.tensor_tensor(hT[q][:, :], sg[q][:, :], psU[q][:, :], ALU.mult))
                need(PE, h, acc_before)
                for j in range(4):
                    last = PE.matmul(psO[q][:, j * P:(j + 1) * P], hT[q][:, j * P:(j + 1) * P],
                                     wbuf[p][:, 2, :], start=True, stop=True)
                d = down.mark(last)
                return d

            def add(e, g, q, d):
                need(DVE, d)
                for j in range(4):
                    t = 4 * g + j
                    last = DVE.scalar_tensor_tensor(out=x[:, t, :], in0=psO[q][:, j * P:(j + 1) * P],
                                                    scalar=wtab[:, t, bass.ds(e, 1)], in1=x[:, t, :],
                                                    op0=ALU.mult, op1=ALU.add)
                return acc.mark(last)

            load(0, 0)
            load(1, 1)
            need(PE, ready)
            need(DVE, *([ready]))
            gate_up(0, 0, 0, (None, 0), (None, 0), ld[0].now())

            def body(i, last_pair):
                G = [gate.now()]
                U = [up.now()]
                SI, HI, AC = [silu.now()], [hid.now()], [acc.now()]
                DN = [down.now()]
                loaded1 = ld[1].now()
                for s in range(8):
                    p, g, q = s // 4, s % 4, s % 2
                    e = i * 2 + p
                    last_step = last_pair and s == 7
                    if not last_step:
                        n = s + 1
                        if n == 4:
                            hl = loaded1
                        elif n == 8:
                            hl = ld[0].now()
                        else:
                            hl = (None, 0)
                        gate_up(0 if n in range(4) or n == 8 else 1, n % 4, n % 2, SI[-1], HI[-1], hl)
                        G.append(gate.now())
                        U.append(up.now())
                    d = finish(e, p, g, q, G[s], U[s], HI[-2] if len(HI) > 1 else HI[0],
                               DN[-2] if len(DN) > 1 else DN[0], AC[-2] if len(AC) > 1 else AC[0])
                    SI.append(silu.now())
                    HI.append(hid.now())
                    DN.append(d)
                    AC.append(add(e, g, q, d))
                    if s in (3, 7) and not last_pair:
                        load(i * 2 + 2 + p, p)

            with loop(nc, E // 2 - 1, {gate: 8, up: 8, down: 8, silu: 8, hid: 8, acc: 8, ld[0]: 1, ld[1]: 1}) as i:
                body(i, False)
            body(E // 2 - 1, True)

        r = {n: sb(f"r_{n}", [P, NT, 32]) for n in ("a", "b", "c", "d")}
        top = sb("top", [P, NT, 8])
        topi = sb("topi", [P, NT, 8], U32)
        topf = sb("topf", [P, NT, 8])
        red = {n: sb(f"red_{n}", [P, NT]) for n in ("a", "b", "c", "d")}

        def chained(tr, engine, instruction):
            v = tr.mark(instruction)
            need(engine, v)
            return v

        def logits(W, E, xT_at, tag):
            pe = track("route_logits")
            need(PE, xT_at)
            for t in range(NT):
                last = PE.matmul(bank[2][:, t * E:(t + 1) * E], xnT[:, t * P:(t + 1) * P], W[:, :],
                                 start=True, stop=True)
            return pe.mark(last)

        def bcast(ap2, n):
            return ap2.unsqueeze(2).broadcast_to([P, NT, n])

        def top_mask(tr, scores, E, k, mask, tmp):
            for t in range(NT):
                v = tr.mark(DVE.max(out=top[:, t, :], in_=scores[:, t, 0:E]))
            need(DVE, v)
            for t in range(NT):
                v = tr.mark(DVE.max_index(out=topi[:, t, :], in_max=top[:, t, :], in_values=scores[:, t, 0:E]))
            need(DVE, v)
            chained(tr, DVE, DVE.tensor_copy(topf[:, :, :], topi[:, :, :]))
            io = iota_e[:, 0:E].unsqueeze(1).broadcast_to([P, NT, E])
            for n in range(k):
                dst = mask if n == 0 else tmp
                chained(tr, DVE, DVE.tensor_tensor(dst[:, :, 0:E], io, bcast(topf[:, :, n], E), ALU.is_equal))
                if n:
                    chained(tr, DVE, DVE.tensor_tensor(mask[:, :, 0:E], mask[:, :, 0:E], tmp[:, :, 0:E], ALU.add))

        def ffn0(tag):
            E = 8
            CENTER, LOWER, UPPER = 1.0 / math.e, 0.5 - math.log(4.0 / 3.0), 0.5
            xT = layernorm_T()
            dv, ac = track(f"route_dve"), track(f"route_act")
            lg = logits(Wr0, E, xT, tag)
            z, inh, w, fb = (r[n][:, :, 0:E] for n in "abcd")
            ps = bank[2][:, 0:NT * E].rearrange("p (t e) -> p t e", e=E)
            need(DVE, lg)
            v = dv.mark(DVE.tensor_scalar(z, ps, temp[:, 0:1], None, ALU.mult))
            need(SCL, v)
            v = ac.mark(SCL.activation(z, z, ACT.Exp, scale=-1.0))
            need(DVE, v)
            c = lambda ins: chained(dv, DVE, ins)
            c(DVE.tensor_scalar(z, z, 1.0, None, ALU.add))
            c(DVE.reciprocal(inh, z))
            c(DVE.tensor_scalar(z, inh, CENTER, None, ALU.subtract))
            c(DVE.tensor_scalar(w, z, -1.0, None, ALU.mult))
            v = c(DVE.tensor_tensor(z, z, w, ALU.max))
            need(SCL, v)
            ac.mark(SCL.activation(w, z, ACT.Exp, scale=-10.0))
            v = ac.mark(SCL.activation(fb, z, ACT.Exp, scale=-1.0 / 0.3))
            need(DVE, v)
            c(DVE.tensor_scalar(z, inh, LOWER, None, ALU.is_ge))
            c(DVE.tensor_tensor(w, w, z, ALU.mult))
            c(DVE.tensor_scalar(z, inh, UPPER, None, ALU.is_le))
            c(DVE.tensor_tensor(w, w, z, ALU.mult))
            c(DVE.tensor_reduce(out=red["a"][:, :], in_=w, axis=AX, op=ALU.add))
            c(DVE.tensor_scalar(red["a"][:, :], red["a"][:, :], 1e-8, None, ALU.is_lt))
            c(DVE.tensor_scalar(red["b"][:, :], red["a"][:, :], -1.0, 1.0, ALU.mult, ALU.add))
            top_mask(dv, r["d"], E, 2, r["a"], r["b"])
            c(DVE.tensor_tensor(fb, fb, z, ALU.mult))
            c(DVE.tensor_reduce(out=red["c"][:, :], in_=fb, axis=AX, op=ALU.add))
            c(DVE.tensor_scalar(red["c"][:, :], red["c"][:, :], 1e-8, None, ALU.max))
            c(DVE.reciprocal(red["c"][:, :], red["c"][:, :]))
            c(DVE.tensor_tensor(red["c"][:, :], red["c"][:, :], red["a"][:, :], ALU.mult))
            c(DVE.tensor_tensor(fb, fb, bcast(red["c"][:, :], E), ALU.mult))
            c(DVE.tensor_tensor(w, w, bcast(red["b"][:, :], E), ALU.mult))
            c(DVE.tensor_tensor(w, w, fb, ALU.add))
            c(DVE.tensor_reduce(out=red["c"][:, :], in_=w, axis=AX, op=ALU.add))
            c(DVE.tensor_scalar(red["c"][:, :], red["c"][:, :], 1e-8, None, ALU.max))
            c(DVE.reciprocal(red["c"][:, :], red["c"][:, :]))
            c(DVE.tensor_scalar(red["c"][:, :], red["c"][:, :], 0.5, None, ALU.mult))
            v = c(DVE.tensor_tensor(wtab[:, :, 0:E], w, bcast(red["c"][:, :], E), ALU.mult))
            expert_loop(E, a["ffn0_w"], tag, v)

        def ffn1(tag):
            E = 32
            xT = layernorm_T()
            dv, ac = track(f"route_dve"), track(f"route_act")
            lg = logits(Wr1, E, xT, tag)
            z, w, sc = (r[n][:, :, :] for n in "abd")
            ps = bank[2][:, 0:NT * E].rearrange("p (t e) -> p t e", e=E)
            need(DVE, lg)
            c = lambda ins: chained(dv, DVE, ins)
            c(DVE.tensor_tensor(z, ps, rbias[:, :].unsqueeze(1).broadcast_to([P, NT, E]), ALU.add))
            c(DVE.tensor_reduce(out=red["a"][:, :], in_=z, axis=AX, op=ALU.max))
            v = c(DVE.tensor_tensor(z, z, bcast(red["a"][:, :], E), ALU.subtract))
            need(SCL, v)
            v = ac.mark(SCL.activation(z, z, ACT.Exp))
            need(DVE, v)
            c(DVE.tensor_reduce(out=red["a"][:, :], in_=z, axis=AX, op=ALU.add))
            c(DVE.reciprocal(red["a"][:, :], red["a"][:, :]))
            c(DVE.tensor_tensor(sc, z, bcast(red["a"][:, :], E), ALU.mult))
            top_mask(dv, r["d"], E, 4, r["a"], r["b"])
            c(DVE.tensor_tensor(sc, sc, z, ALU.mult))
            c(DVE.tensor_reduce(out=red["a"][:, :], in_=sc, axis=AX, op=ALU.add))
            c(DVE.tensor_scalar(red["a"][:, :], red["a"][:, :], 1e-12, None, ALU.max))
            c(DVE.reciprocal(red["a"][:, :], red["a"][:, :]))
            c(DVE.tensor_scalar(red["a"][:, :], red["a"][:, :], 0.5, None, ALU.mult))
            c(DVE.tensor_tensor(wtab[:, :, 0:E], sc, bcast(red["a"][:, :], E), ALU.mult))
            v = c(DVE.memset(wtab[:, :, E:E + 4], 0.5))
            expert_loop(E + 4, a["ffn1_w"], tag, v)

        H, HD, M = 16, 8, 64
        NP2 = H // 2
        R = S // M
        qT, kT, svT = sb("qT", [P, S]), sb("kT", [P, S]), sb("svT", [P, S])
        v_sb = sb("v_sb", [P, TB, D])
        klm, qlm = sb("klm", [P, M]), sb("qlm", [P, M])
        KB, QB = sb("KB", [P, H, M]), sb("QB", [P, H, M])
        E1 = sb("E1", [P, H, M])
        E1T = sb("E1T", [P, NP2, S])
        m1, s1 = sb("m1", [P, H]), sb("s1", [P, TB, H])
        E3 = [sb(f"E3_{p}", [P, S]) for p in range(2)]
        E3T = [sb(f"E3T_{p}", [P, S]) for p in range(2)]
        m3, s3 = sb("m3", [P, NP2]), sb("s3", [P, NP2])
        Kc, Kbd, KTbd = sb("Kc", [P, NP2, M]), sb("Kbd", [P, NP2, P]), sb("KTbd", [P, NP2, P])
        KTc = sb("KTc", [P, NP2, M])
        m2, s2, rden = sb("m2", [P, NP2]), sb("s2", [P, NP2]), sb("rden", [P, NP2])
        Ac, Tc = sb("Ac", [P, NP2, M]), sb("Tc", [P, NP2, M])
        Abd, Pbd = sb("Abd", [P, NP2, P]), sb("Pbd", [P, NP2, P])
        y = sb("y", [P, NP2, HD])
        WB = sb("WB", [P, NP2, 2 * HD])
        sv = sb("sv", [P, TB, D])
        xbT = sb("xbT", [P, S])
        I7, I15, I13 = sb("I7", [P, M]), sb("I15", [P, M]), sb("I13", [P, M])

        def pairs(ap2):
            return ap2.unsqueeze(1).broadcast_to([P, NP2, M])

        def attn0():
            pe, dv, ac = track("a0_pe"), track("a0_dve"), track("a0_act")
            need(SCL, layernorm_T())

            def V(ins):
                return chained(dv, DVE, ins)

            def A(ins):
                return chained(ac, SCL, ins)

            for t in (Kbd, Abd, Pbd):
                V(DVE.memset(t[:, :, :], 0.0))
            V(DVE.memset(WB[:, :, :], 0.0))
            for t, f in ((I7, 7.0), (I15, 15.0), (I13, 3.25)):
                V(DVE.tensor_scalar(t[:, :], ident2[:, :], f, None, ALU.mult))

            def to_blocks(dst, src, n=M):
                V(DVE.tensor_copy(dst[0:64, :, 0:n], src[0:64]))
                return V(DVE.tensor_copy(dst[64:P, :, n:2 * n], src[64:P]))

            def pv(b):
                return b[:, :].rearrange("p (k m) -> p k m", m=M)

            def batch(b):
                need(SCL, pe.now(), dv.now())
                A(SCL.copy(xbT[:, :], xnT[:, bass.ds(b * S, S)]))
                need(PE, ac.now())
                PE.matmul(bank[1][:, :], wqkv[:, 0:D], xbT[:, :], start=True, stop=True)
                PE.matmul(bank[2][:, :], wqkv[:, D:2 * D], xbT[:, :], start=True, stop=True)
                for j in range(TB):
                    last = PE.matmul(bank[3][:, j * P:(j + 1) * P], xbT[:, j * P:(j + 1) * P], wqkv[:, 2 * D:3 * D],
                                     start=True, stop=True)
                need(SCL, pe.mark(last))
                A(SCL.mul(qT[:, :], bank[1][:, :], HD ** -0.5))
                A(SCL.copy(kT[:, :], bank[2][:, :]))
                A(SCL.copy(v_sb[:, :, :], bank[3][:, :].rearrange("p (j d) -> p j d", d=D)))
                need(DVE, ac.now())
                for src, lm, dst in ((qT, qlm, QB), (kT, klm, KB)):
                    V(DVE.tensor_reduce(out=lm[:, :], in_=src[:, :].rearrange("p (m r) -> p m r", r=R), axis=AX, op=ALU.add))
                    V(DVE.tensor_scalar(lm[:, :], lm[:, :], 1.0 / R, None, ALU.mult))
                    V(DVE.tensor_tensor(dst[:, :, :], lm[:, :].unsqueeze(1).broadcast_to([P, H, M]),
                                        headmask[:, :].unsqueeze(2).broadcast_to([P, H, M]), ALU.mult))

                need(PE, dv.now())
                for k in range(NP2):
                    last = PE.matmul(bank[0][:, k * M:(k + 1) * M], QB[:, 2 * k:2 * k + 2, :], klm[:, :], start=True, stop=True)
                need(DVE, pe.mark(last))
                V(DVE.tensor_reduce(out=m2[:, :], in_=pv(bank[0]), axis=AX, op=ALU.max))
                V(DVE.tensor_tensor(Kc[:, :, :], pv(bank[0]), m2[:, :].unsqueeze(2).broadcast_to([P, NP2, M]), ALU.subtract))
                need(SCL, dv.now())
                A(SCL.activation(Kc[:, :, :], Kc[:, :, :], ACT.Exp))
                need(DVE, ac.now())
                V(DVE.tensor_reduce(out=s2[:, :], in_=Kc[:, :, :], axis=AX, op=ALU.add))
                V(DVE.reciprocal(s2[:, :], s2[:, :]))
                V(DVE.tensor_tensor(Kc[:, :, :], Kc[:, :, :], s2[:, :].unsqueeze(2).broadcast_to([P, NP2, M]), ALU.mult))
                to_blocks(Kbd, Kc)
                need(PE, dv.now(), ac.now())
                PE.matmul(bank[0][:, :], blockones[:, :], Kc[:, :, :], start=True, stop=True)
                for k in range(NP2):
                    last = PE.transpose(bank[1 + k // 4][:, k % 4 * P:(k % 4 + 1) * P], Kbd[:, k, :], ident[:, :])
                need(DVE, pe.mark(last))
                V(DVE.tensor_reduce(out=rden[:, :], in_=pv(bank[0]), axis=AX, op=ALU.max))
                V(DVE.reciprocal(rden[:, :], rden[:, :]))
                for h in range(2):
                    V(DVE.tensor_copy(KTbd[:, 4 * h:4 * h + 4, :], bank[1 + h][:, :].rearrange("p (k m) -> p k m", m=P)))
                V(DVE.tensor_copy(KTc[0:64, :, :], KTbd[0:64, :, 0:64]))
                V(DVE.tensor_copy(KTc[64:P, :, :], KTbd[64:P, :, 64:P]))
                need(PE, dv.now())
                for k in range(NP2):
                    last = PE.matmul(bank[0][:, k * M:(k + 1) * M], KTbd[:, k, :], KTc[:, k, :], start=True, stop=True)
                need(DVE, pe.mark(last))
                V(DVE.tensor_tensor(Ac[:, :, :], pv(bank[0]), rden[:, :].unsqueeze(2).broadcast_to([P, NP2, M]), ALU.mult))

                for k in range(NP2):
                    q = k % 2
                    need(PE, dv.now(), ac.now())
                    need(DVE, pe.mark(PE.matmul(bank[2][:, :], QB[:, 2 * k:2 * k + 2, :], kT[:, :], start=True, stop=True)))
                    V(DVE.tensor_reduce(out=m3[:, k:k + 1], in_=bank[2][:, :], axis=AX, op=ALU.max, negate=True))
                    need(SCL, dv.now())
                    A(SCL.activation(E3[q][:, :], bank[2][:, :], ACT.Exp, bias=m3[:, k:k + 1], accum_out=s3[:, k:k + 1]))
                    need(PE, ac.now())
                    for j in range(TB):
                        last = PE.transpose(bank[3][:, j * P:(j + 1) * P], E3[q][:, j * P:(j + 1) * P], ident[:, :])
                    need(SCL, pe.mark(last))
                    A(SCL.copy(E3T[q][:, :], bank[3][:, :]))
                    need(PE, ac.now())
                    for j in range(TB):
                        last = PE.matmul(bank[4][:, k * 16:(k + 1) * 16], E3T[q][:, j * P:(j + 1) * P],
                                         v_sb[:, j, k * 16:(k + 1) * 16], start=(j == 0), stop=(j == TB - 1))
                    pe.mark(last)
                need(DVE, pe.now(), ac.now())
                V(DVE.reciprocal(s3[:, :], s3[:, :]))
                kv = bank[4][:, 0:P].rearrange("p (k d) -> p k d", d=2 * HD)
                for h in range(2):
                    rows = slice(64 * h, 64 * h + 64)
                    V(DVE.tensor_tensor(y[rows, :, :], kv[rows, :, HD * h:HD * h + HD],
                                        s3[rows, :].unsqueeze(2).broadcast_to([64, NP2, HD]), ALU.mult))

                for n in range(6):
                    to_blocks(Abd, Ac)
                    V(DVE.scalar_tensor_tensor(out=Tc[:, :, :], in0=Ac[:, :, :], scalar=-1.0, in1=pairs(I7[:, :]),
                                               op0=ALU.mult, op1=ALU.add))
                    for c, diag in ((-1.0, I15), (-0.25, I13)):
                        need(PE, dv.now())
                        for k in range(NP2):
                            last = PE.matmul(bank[0][:, k * M:(k + 1) * M], Abd[:, k, :], Tc[:, k, :], start=True, stop=True)
                        need(DVE, pe.mark(last))
                        V(DVE.scalar_tensor_tensor(out=Tc[:, :, :], in0=pv(bank[0]), scalar=c, in1=pairs(diag[:, :]),
                                                   op0=ALU.mult, op1=ALU.add))
                    to_blocks(Pbd, Tc)
                    need(PE, dv.now())
                    for k in range(NP2):
                        last = PE.matmul(bank[1][:, k * HD:(k + 1) * HD], Pbd[:, k, :], y[:, k, :], start=True, stop=True)
                    if n < 5:
                        for k in range(NP2):
                            last = PE.matmul(bank[0][:, k * M:(k + 1) * M], Abd[:, k, :], Tc[:, k, :], start=True, stop=True)
                    need(DVE, pe.mark(last))
                    V(DVE.tensor_copy(y[:, :, :], bank[1][:, 0:64].rearrange("p (k d) -> p k d", d=HD)))
                    if n < 5:
                        V(DVE.tensor_copy(Ac[:, :, :], pv(bank[0])))
                need(PE, dv.now())
                for k in range(NP2):
                    last = PE.matmul(bank[1][:, k * HD:(k + 1) * HD], Kbd[:, k, :], y[:, k, :], start=True, stop=True)
                need(DVE, pe.mark(last))
                kv = bank[1][:, 0:64].rearrange("p (k d) -> p k d", d=HD)
                for h in range(2):
                    rows = slice(64 * h, 64 * h + 64)
                    V(DVE.tensor_tensor(WB[rows, :, HD * h:HD * h + HD], kv[rows, :, :],
                                        rden[rows, :].unsqueeze(2).broadcast_to([64, NP2, HD]), ALU.mult))

                for j in range(TB):
                    need(PE, dv.now(), ac.now())
                    for h in range(2):
                        last = PE.matmul(bank[2 + h][:, :], qT[:, j * P:(j + 1) * P], KB[:, 8 * h:8 * h + 8, :], start=True, stop=True)
                    need(DVE, pe.mark(last))
                    for h in range(2):
                        hs = slice(8 * h, 8 * h + 8)
                        V(DVE.tensor_reduce(out=m1[:, hs], in_=pv(bank[2 + h]), axis=AX, op=ALU.max))
                        V(DVE.tensor_tensor(E1[:, hs, :], pv(bank[2 + h]), m1[:, hs].unsqueeze(2).broadcast_to([P, 8, M]), ALU.subtract))
                    need(SCL, dv.now())
                    A(SCL.activation(E1[:, :, :], E1[:, :, :], ACT.Exp))
                    need(DVE, ac.now())
                    V(DVE.tensor_reduce(out=s1[:, j, :], in_=E1[:, :, :], axis=AX, op=ALU.add))
                    need(PE, dv.now(), ac.now())
                    for h in range(2):
                        for k in range(4):
                            last = PE.transpose(bank[4 + h][:, k * P:(k + 1) * P], E1[:, 2 * (4 * h + k):2 * (4 * h + k) + 2, :], ident[:, :])
                    need(SCL, pe.mark(last))
                    for h in range(2):
                        A(SCL.copy(E1T[:, 4 * h:4 * h + 4, j * P:(j + 1) * P], bank[4 + h][:, :].rearrange("p (k t) -> p k t", t=P)))
                V(DVE.reciprocal(s1[:, :, :], s1[:, :, :]))
                need(PE, dv.now(), ac.now())
                for j in range(TB):
                    for k in range(NP2):
                        last = PE.matmul(bank[0][:, j * P + k * 16:j * P + (k + 1) * 16], E1T[:, k, j * P:(j + 1) * P], WB[:, k, :],
                                         start=True, stop=True)
                need(DVE, pe.mark(last))
                V(DVE.tensor_tensor(sv[:, :, :].rearrange("p j (h d) -> p (j h) d", d=HD),
                                    bank[0][:, :].rearrange("p (g d) -> p g d", d=HD),
                                    s1[:, :, :].rearrange("p j h -> p (j h)").unsqueeze(2).broadcast_to([P, TB * H, HD]), ALU.mult))
                need(PE, dv.now())
                for j in range(TB):
                    last = PE.transpose(bank[1][:, j * P:(j + 1) * P], sv[:, j, :], ident[:, :])
                need(SCL, pe.mark(last))
                A(SCL.copy(svT[:, :], bank[1][:, :]))
                need(PE, ac.now())
                for j in range(TB):
                    last = PE.matmul(bank[2][:, j * P:(j + 1) * P], svT[:, j * P:(j + 1) * P], wproj[:, :], start=True, stop=True)
                need(DVE, pe.mark(last))
                xs = x[:, bass.ds(b * TB, TB), :]
                dv.mark(DVE.tensor_tensor(xs, bank[2][:, :].rearrange("p (j d) -> p j d", d=D), xs, ALU.add))
                need(DVE, dv.now())

            marks = CNT["attn0"]
            with loop(nc, B, {pe: marks[0], dv: marks[1], ac: marks[2]}) as b:
                batch(b)
            return dv.now(), ac.now(), pe.now()

        NW = 2 * S // P - 1
        vw = sb("vw", [P, NW, D])
        Ew = [sb(f"Ew{p}", [P, P]) for p in range(2)]
        EwT = [sb(f"EwT{p}", [P, P]) for p in range(2)]
        mw, sw = sb("mw", [P, NW]), sb("sw", [P, NW])

        def attn1():
            pe, dv, ac = track("a1_pe"), track("a1_dve"), track("a1_act")
            need(SCL, layernorm_T())
            SC = 1.0 / math.sqrt(8.0)

            def V(ins):
                return chained(dv, DVE, ins)

            def A(ins):
                return chained(ac, SCL, ins)

            def batch(b):
                need(SCL, pe.now(), dv.now())
                A(SCL.copy(xbT[:, :], xnT[:, bass.ds(b * S, S)]))
                need(PE, ac.now())
                PE.matmul(bank[1][:, :], wq1[:, :], xbT[:, :], start=True, stop=True)
                PE.matmul(bank[2][:, :], wk1[:, :], xbT[:, :], start=True, stop=True)
                for w in range(NW):
                    last = PE.matmul(bank[3 + w // 4][:, w % 4 * P:(w % 4 + 1) * P], xbT[:, w * 64:w * 64 + P], wv1[:, :],
                                     start=True, stop=True)
                need(SCL, pe.mark(last))
                need(DVE, pe.now())
                A(SCL.activation(qT[:, :], bank[1][:, :], ACT.Identity, bias=bq1[:, 0:1]))
                A(SCL.activation(kT[:, :], bank[2][:, :], ACT.Identity, bias=bk1[:, 0:1]))
                for g, n in ((0, 4), (1, NW - 4)):
                    V(DVE.tensor_tensor(vw[:, 4 * g:4 * g + n, :], bank[3 + g][:, 0:n * P].rearrange("p (w d) -> p w d", d=D),
                                        bv1[:, :].unsqueeze(1).broadcast_to([P, n, D]), ALU.add))
                for n, w in enumerate([0, 2, 4, 6, 1, 3, 5]):
                    q = n % 2
                    win = slice(w * 64, w * 64 + P)
                    need(PE, dv.now(), ac.now())
                    need(DVE, pe.mark(PE.matmul(bank[6][:, 0:P], qT[:, win], kT[:, win], start=True, stop=True)))
                    V(DVE.tensor_reduce(out=mw[:, w:w + 1], in_=bank[6][:, 0:P], axis=AX, op=ALU.max))
                    V(DVE.tensor_scalar(mw[:, w:w + 1], mw[:, w:w + 1], -SC, None, ALU.mult))
                    need(SCL, dv.now())
                    A(SCL.activation(Ew[q][:, :], bank[6][:, 0:P], ACT.Exp, bias=mw[:, w:w + 1], scale=SC, accum_out=sw[:, w:w + 1]))
                    need(DVE, ac.now())
                    V(DVE.reciprocal(sw[:, w:w + 1], sw[:, w:w + 1]))
                    V(DVE.tensor_scalar(Ew[q][:, :], Ew[q][:, :], sw[:, w:w + 1], None, ALU.mult))
                    need(PE, dv.now())
                    need(SCL, pe.mark(PE.transpose(bank[0][:, 0:P], Ew[q][:, :], ident[:, :])))
                    A(SCL.copy(EwT[q][:, :], bank[0][:, 0:P]))
                    need(PE, ac.now())
                    pe.mark(PE.matmul(bank[7][:, win], vw[:, w, :], EwT[q][:, :], start=(n == 0), stop=(n == NW - 1),
                                      skip_group_check=True))
                need(SCL, pe.now())
                A(SCL.copy(svT[:, 0:64], bank[7][:, 0:64]))
                A(SCL.mul(svT[:, 64:S - 64], bank[7][:, 64:S - 64], 0.5))
                A(SCL.copy(svT[:, S - 64:S], bank[7][:, S - 64:S]))
                need(PE, ac.now())
                for j in range(TB):
                    last = PE.matmul(bank[1][:, j * P:(j + 1) * P], svT[:, j * P:(j + 1) * P], wo1[:, :], start=True, stop=True)
                need(DVE, pe.mark(last))
                xs = x[:, bass.ds(b * TB, TB), :]
                V(DVE.tensor_tensor(xs, bank[1][:, :].rearrange("p (j d) -> p j d", d=D), xs, ALU.add))
                V(DVE.tensor_tensor(xs, xs, bo1[:, :].unsqueeze(1).broadcast_to([P, TB, D]), ALU.add))

            marks = CNT["attn1"]
            with loop(nc, B, {pe: marks[0], dv: marks[1], ac: marks[2]}) as b:
                batch(b)
            return dv.now(), ac.now(), pe.now()

        ffn0("f0a")
        attn0()
        ffn0("f0b")
        ffn1("f1a")
        attn1()
        ffn1("f1b")
        s_out = track("stored", 16)
        need(SP, s_res.now())
        s_out.mark(SP.dma_start(out.rearrange("b (t p) d -> p (b t) d", p=P), x[:, :, :]))
        need(SP, s_out.now())


LOOP_TRACKS = ("expert_load0 expert_load1 expert_gate expert_up expert_down expert_silu expert_hidden x_updated "
               "a0_pe a0_dve a0_act a1_pe a1_dve a1_act").split()
CNT = {"attn0": (58, 109, 34), "attn1": (23, 32, 20)}

_X = "x wqkv wproj Wr temp WrT rbias Wq Wk Wv Wo bq bk bv bo ffn0_w ffn1_w".split()


def kernel(**inputs):
    import numpy as _np
    import concourse.bacc as _bacc
    from concourse import mybir as _mybir
    from concourse.bass_utils import run_bass_kernel_spmd as _run

    i = {k: _np.asarray(v) for k, v in inputs.items()}
    t = lambda w: w.transpose(0, 2, 1)
    rows = lambda w: w.reshape(4, P, w.shape[1])
    g0, u0, d0 = (i[f"L0_ffn_{n}"] for n in ("Wg", "Wu", "Wd"))
    g1 = _np.concatenate([t(i["L1_ffn_gate_w"]), t(rows(i["L1_ffn_sgate_w"]))])
    u1 = _np.concatenate([t(i["L1_ffn_up_w"]), t(rows(i["L1_ffn_sup_w"]))])
    d1 = _np.concatenate([t(i["L1_ffn_down_w"]), i["L1_ffn_sdown_w"].T.reshape(4, P, P)])
    a = {
        "x": i["L0_attn_x"], "wqkv": i["L0_attn_w_qkv"], "wproj": i["L0_attn_w_proj"],
        "Wr": i["L0_ffn_Wr"], "temp": i["L0_ffn_temperature"],
        "WrT": i["L1_ffn_router_w"].T, "rbias": i["L1_ffn_router_bias"],
        "Wq": i["L1_attn_Wq"], "Wk": i["L1_attn_Wk"], "Wv": i["L1_attn_Wv"], "Wo": i["L1_attn_Wo"],
        "bq": i["L1_attn_bq"], "bk": i["L1_attn_bk"], "bv": i["L1_attn_bv"], "bo": i["L1_attn_bo"],
        "ffn0_w": _np.stack([g0, u0, d0], axis=2),
        "ffn1_w": _np.stack([g1, u1, d1], axis=2),
    }
    nc = _bacc.Bacc("TRN2", target_bir_lowering=False, num_devices=1)
    arrays, aps = {}, {}
    for name in _X:
        v = _np.ascontiguousarray(a[name])
        arrays[f"in_{name}"] = v
        aps[name] = nc.dram_tensor(f"in_{name}", v.shape, _mybir.dt.from_np(v.dtype), kind="ExternalInput").ap()
    out = nc.dram_tensor("out", a["x"].shape, _mybir.dt.float32, kind="ExternalOutput").ap()
    build(nc, aps, out)
    return _run(nc, [arrays], core_ids=[0]).results[0]["out"]
```

```python
import math
from contextlib import ExitStack, contextmanager

import numpy as np
import concourse.bass as bass
from concourse import mybir

F32 = mybir.dt.float32
U32 = mybir.dt.uint32
ALU = mybir.AluOpType
ACT = mybir.ActivationFunctionType
AX = mybir.AxisListType.X
P = 128


class Track:

    def __init__(self, sem, step=1):
        self.sem, self.step = sem, step
        self.base, self.local, self.per_iter, self.i = 0, 0, None, None

    def now(self):
        if self.i is None:
            return self.sem, self.base + self.local
        return self.sem, self.i * self.per_iter + (self.base + self.local)

    def mark(self, instruction):
        instruction.then_inc(self.sem, self.step)
        self.local += self.step
        return self.now()


def need(engine, *values):
    for sem, value in values:
        if sem is not None and not (isinstance(value, int) and value <= 0):
            engine.wait_ge(sem, value)


def skew(n, *stages):
    for t in range(n + len(stages) - 1):
        for k, stage in enumerate(stages):
            if 0 <= t - k < n:
                stage(t - k)


@contextmanager
def loop(nc, count, marks):
    with nc.Fori(0, count) as i:
        for t, n in marks.items():
            t.base, t.local, t.per_iter, t.i = t.base + t.local, 0, n * t.step, i
        yield i
        wrong = {t.sem.name: t.local // t.step for t, n in marks.items() if t.local != n * t.step}
        assert not wrong, f"marks per iteration: {wrong}"
        for t in marks:
            t.base, t.local, t.i = t.base + count * t.per_iter, 0, None


def build(nc, a, out):
    B, S, D = a["x"].shape
    T = B * S
    NT = T // P
    TB = S // P
    GW = 4 * P
    NG = T // GW
    PE, DVE, SCL, POOL, SP = nc.tensor, nc.vector, nc.scalar, nc.gpsimd, nc.sync

    with ExitStack() as ctx:
        tracks = {}

        def sb(name, shape, dt=F32):
            return ctx.enter_context(nc.sbuf_tensor(name, shape, dt))

        def track(name, step=1):
            if name not in tracks:
                tracks[name] = Track(ctx.enter_context(nc.semaphore(name)), step)
            return tracks[name]

        for name in LOOP_TRACKS:
            t = track(name, 16 if "load" in name else 1)
            SP.sem_inc(t.sem, t.step)
            t.local = t.step
        nc.all_engine_barrier()

        bank = [ctx.enter_context(nc.psum_tensor(f"bank{n}", [P, 512], F32)) for n in range(8)]

        x = sb("x", [P, NT, D])
        xn = sb("xn", [P, NT, D])
        xnT = sb("xnT", [P, T])
        ident = sb("ident", [P, P])
        ident2 = sb("ident2", [P, 64])
        headmask = sb("headmask", [P, 16])
        blockones = sb("blockones", [P, P])
        iota_e = sb("iota_e", [P, 32])
        stats = sb("stats", [P, NT, 6])
        mv = sb("mv", [P, NT, 2])
        rstd = sb("rstd", [P, NT])

        s_x = track("x_loaded", 16)
        s_w = track("small_loaded", 16)
        s_c = track("const_pool")
        s_cv = track("const_dve")

        xr = a["x"].rearrange("b (t p) d -> p (b t) d", p=P)
        s_x.mark(SP.dma_start(x[:, :, :], xr))

        def load(name, shape, src):
            t = sb(name, shape)
            s_w.mark(SCL.dma_start(t[:], src))
            return t

        Wr0 = load("Wr0", [D, 8], a["Wr"])
        temp = load("temp", [P, 1], a["temp"].rearrange("(o a) -> o a", o=1).broadcast_to([P, 1]))
        wqkv = load("wqkv", [D, 3 * D], a["wqkv"])
        wproj = load("wproj", [D, D], a["wproj"])
        Wr1 = load("Wr1", [D, 32], a["WrT"])
        rbias = load("rbias", [P, 32], a["rbias"].rearrange("(o a) -> o a", o=1).broadcast_to([P, 32]))
        wq1, wk1, wv1, wo1 = (load(n, [D, D], a[n]) for n in ("Wq", "Wk", "Wv", "Wo"))
        bq1, bk1 = (load(n, [D, 1], a[n].rearrange("(d o) -> d o", o=1)) for n in ("bq", "bk"))
        bv1, bo1 = (load(n, [P, D], a[n].rearrange("(o d) -> o d", o=1).broadcast_to([P, D])) for n in ("bv", "bo"))

        s_c.mark(POOL.memset(ident[:, :], 0.0))
        s_c.mark(POOL.memset(ident2[:, :], 0.0))
        s_c.mark(POOL.memset(headmask[:, :], 1.0))
        s_c.mark(POOL.iota(iota_e[:, :], pattern=[[1, 32]], base=0, channel_multiplier=0,
                           allow_small_or_imprecise_dtypes=True))
        need(POOL, s_c.now())
        s_c.mark(POOL.affine_select(out=ident[:, :], in_=ident[:, :], compare_op=ALU.not_equal, fill=1.0,
                                    base=0, pattern=[[-1, P]], channel_multiplier=1))
        for base in (0, -64):
            s_c.mark(POOL.affine_select(out=ident2[:, :], in_=ident2[:, :], compare_op=ALU.not_equal, fill=1.0,
                                        base=base, pattern=[[-1, 64]], channel_multiplier=1))
            need(POOL, s_c.now())
        s_c.mark(POOL.affine_select(out=headmask[:, :], in_=headmask[:, :], compare_op=ALU.is_ge, fill=0.0,
                                    base=0, pattern=[[-8, 16]], channel_multiplier=1))
        need(POOL, s_c.now())
        s_c.mark(POOL.affine_select(out=headmask[:, :], in_=headmask[:, :], compare_op=ALU.is_ge, fill=0.0,
                                    base=7, pattern=[[8, 16]], channel_multiplier=-1))
        mhalf = sb("mhalf", [P, NT])
        s_c.mark(POOL.memset(mhalf[:, :], -0.5))
        s_cv.mark(DVE.memset(blockones[0:64, 0:64], 1.0))
        s_cv.mark(DVE.memset(blockones[0:64, 64:P], 0.0))
        s_cv.mark(DVE.memset(blockones[64:P, 0:64], 0.0))
        s_cv.mark(DVE.memset(blockones[64:P, 64:P], 1.0))
        need(DVE, s_w.now())
        s_cv.mark(DVE.reciprocal(temp[:, 0:1], temp[:, 0:1]))
        for e in (PE, SCL, DVE):
            need(e, s_c.now(), s_cv.now(), s_w.now(), s_x.now())
        need(POOL, s_cv.now(), s_w.now(), s_x.now())

        s_res = track("x_updated")

        s_ln = {n: track(f"ln_{n}") for n in ("stats", "pow", "norm", "transposed", "evacuated")}

        def layernorm_T(updated, banks=(bank[6], bank[7])):
            done, pow_at = [None] * NG, [None] * NG

            def statistics(g):
                ts = range(4 * g, 4 * g + 4)
                need(DVE, updated[g])
                for t in ts:
                    v = s_ln["stats"].mark(DVE.bn_stats(out=stats[:, t, :], in_=x[:, t, :]))
                need(DVE, v)
                for t in ts:
                    v = s_ln["stats"].mark(DVE.bn_aggr(out=mv[:, t, :], in_=stats[:, t, :]))
                need(DVE, v)
                r = rstd[:, 4 * g:4 * g + 4]
                need(POOL, s_ln["stats"].mark(DVE.tensor_scalar(r, mv[:, 4 * g:4 * g + 4, 1], 1e-5, None, ALU.add)))
                pow_at[g] = s_ln["pow"].mark(POOL.tensor_tensor(r, r, mhalf[:, 4 * g:4 * g + 4], ALU.pow))

            def normalise(g):
                need(DVE, pow_at[g])
                if g == 0:
                    need(DVE, s_ln["transposed"].now())
                for t in range(4 * g, 4 * g + 4):
                    v = s_ln["norm"].mark(DVE.tensor_scalar(xn[:, t, :], x[:, t, :], mv[:, t, 0:1], rstd[:, t:t + 1],
                                                            ALU.subtract, ALU.mult))
                b = banks[g % 2]
                need(PE, v, updated[g], done[g - 2] if g > 1 else (None, 0))
                for t in range(4 * g, 4 * g + 4):
                    last = PE.transpose(b[:, t % 4 * P:(t % 4 + 1) * P], xn[:, t, :], ident[:, :])
                need(SCL, s_ln["transposed"].mark(last))
                done[g] = s_ln["evacuated"].mark(SCL.copy(xnT[:, g * GW:(g + 1) * GW], b[:, :]))

            skew(NG, statistics, normalise)
            return done

        wbuf = [sb(f"wbuf{p}", [P, 3, P]) for p in range(2)]
        sg = [sb(f"sg{p}", [P, GW]) for p in range(2)]
        hT = [sb(f"hT{p}", [P, GW]) for p in range(2)]
        wtab = sb("wtab", [P, NT, 36])

        def expert_loop(E, weights, tag, ready):
            ld = [track(f"expert_load{p}", 16) for p in range(2)]
            gate, up, down = track("expert_gate"), track("expert_up"), track("expert_down")
            silu, hid, acc = track("expert_silu"), track("expert_hidden"), s_res
            psG, psU, psO = bank[0:2], bank[2:4], bank[4:6]

            def load(e, p):
                need(SP, down.now())
                ld[p].mark(SP.dma_start(wbuf[p][:, :, :], weights[bass.ds(e, 1), :, :, :]
                                        .rearrange("o p k n -> p (o k) n")))

            def gate_up(p, g, q, gate_free, up_free, hid_loaded):
                cols = slice(g * GW, (g + 1) * GW)
                need(PE, gate_free, hid_loaded)
                gate.mark(PE.matmul(psG[q][:, :], wbuf[p][:, 0, :], xnT[:, cols], start=True, stop=True))
                need(PE, up_free)
                up.mark(PE.matmul(psU[q][:, :], wbuf[p][:, 1, :], xnT[:, cols], start=True, stop=True))

            def finish(e, p, g, q, gate_at, up_at, sg_free, hT_free, acc_before):
                need(SCL, gate_at, sg_free)
                s = silu.mark(SCL.activation(sg[q][:, :], psG[q][:, :], ACT.Silu))
                need(DVE, s, up_at, hT_free)
                h = hid.mark(DVE.tensor_tensor(hT[q][:, :], sg[q][:, :], psU[q][:, :], ALU.mult))
                need(PE, h, acc_before)
                for j in range(4):
                    last = PE.matmul(psO[q][:, j * P:(j + 1) * P], hT[q][:, j * P:(j + 1) * P],
                                     wbuf[p][:, 2, :], start=True, stop=True)
                d = down.mark(last)
                return d

            def add(e, g, q, d):
                need(DVE, d)
                for j in range(4):
                    t = 4 * g + j
                    last = DVE.scalar_tensor_tensor(out=x[:, t, :], in0=psO[q][:, j * P:(j + 1) * P],
                                                    scalar=wtab[:, t, bass.ds(e, 1)], in1=x[:, t, :],
                                                    op0=ALU.mult, op1=ALU.add)
                return acc.mark(last)

            load(0, 0)
            load(1, 1)
            need(PE, ready)
            need(DVE, *([ready]))
            gate_up(0, 0, 0, (None, 0), (None, 0), ld[0].now())

            def body(i, last_pair):
                G = [gate.now()]
                U = [up.now()]
                SI, HI, AC = [silu.now()], [hid.now()], [acc.now()]
                DN = [down.now()]
                loaded1 = ld[1].now()
                for s in range(8):
                    p, g, q = s // 4, s % 4, s % 2
                    e = i * 2 + p
                    last_step = last_pair and s == 7
                    if not last_step:
                        n = s + 1
                        if n == 4:
                            hl = loaded1
                        elif n == 8:
                            hl = ld[0].now()
                        else:
                            hl = (None, 0)
                        gate_up(0 if n in range(4) or n == 8 else 1, n % 4, n % 2, SI[-1], HI[-1], hl)
                        G.append(gate.now())
                        U.append(up.now())
                    d = finish(e, p, g, q, G[s], U[s], HI[-2] if len(HI) > 1 else HI[0],
                               DN[-2] if len(DN) > 1 else DN[0], AC[max(s - 1, 0)])
                    SI.append(silu.now())
                    HI.append(hid.now())
                    DN.append(d)
                    if s:
                        AC.append(add(*pending))
                    pending = (e, g, q, d)
                    if s == 7:
                        AC.append(add(*pending))
                    if s in (3, 7) and not last_pair:
                        load(i * 2 + 2 + p, p)
                return AC[-NG:]

            with loop(nc, E // 2 - 1, {gate: 8, up: 8, down: 8, silu: 8, hid: 8, acc: 8, ld[0]: 1, ld[1]: 1}) as i:
                body(i, False)
            return body(E // 2 - 1, True)

        r = {n: sb(f"r_{n}", [P, NT, 32]) for n in ("a", "b", "c", "d")}
        top = sb("top", [P, NT, 8])
        topi = sb("topi", [P, NT, 8], U32)
        topf = sb("topf", [P, NT, 8])
        red = {n: sb(f"red_{n}", [P, NT]) for n in ("a", "b", "c", "d")}

        def chained(tr, engine, instruction):
            v = tr.mark(instruction)
            need(engine, v)
            return v

        def logits(W, E, xT_at, tag):
            pe = track("route_logits")
            need(PE, *xT_at)
            for t in range(NT):
                last = PE.matmul(bank[2][:, t * E:(t + 1) * E], xnT[:, t * P:(t + 1) * P], W[:, :],
                                 start=True, stop=True)
            return pe.mark(last)

        def bcast(ap2, n):
            return ap2.unsqueeze(2).broadcast_to([P, NT, n])

        def top_mask(tr, scores, E, k, mask, tmp):
            for t in range(NT):
                v = tr.mark(DVE.max(out=top[:, t, :], in_=scores[:, t, 0:E]))
            need(DVE, v)
            for t in range(NT):
                v = tr.mark(DVE.max_index(out=topi[:, t, :], in_max=top[:, t, :], in_values=scores[:, t, 0:E]))
            need(DVE, v)
            chained(tr, DVE, DVE.tensor_copy(topf[:, :, :], topi[:, :, :]))
            io = iota_e[:, 0:E].unsqueeze(1).broadcast_to([P, NT, E])
            for n in range(k):
                dst = mask if n == 0 else tmp
                chained(tr, DVE, DVE.tensor_tensor(dst[:, :, 0:E], io, bcast(topf[:, :, n], E), ALU.is_equal))
                if n:
                    chained(tr, DVE, DVE.tensor_tensor(mask[:, :, 0:E], mask[:, :, 0:E], tmp[:, :, 0:E], ALU.add))

        def ffn0(tag, updated):
            E = 8
            CENTER, LOWER, UPPER = 1.0 / math.e, 0.5 - math.log(4.0 / 3.0), 0.5
            xT = layernorm_T(updated)
            dv, ac = track(f"route_dve"), track(f"route_act")
            lg = logits(Wr0, E, xT, tag)
            z, inh, w, fb = (r[n][:, :, 0:E] for n in "abcd")
            ps = bank[2][:, 0:NT * E].rearrange("p (t e) -> p t e", e=E)
            need(DVE, lg)
            v = dv.mark(DVE.tensor_scalar(z, ps, temp[:, 0:1], None, ALU.mult))
            need(SCL, v)
            v = ac.mark(SCL.activation(z, z, ACT.Exp, scale=-1.0))
            need(DVE, v)
            c = lambda ins: chained(dv, DVE, ins)
            c(DVE.tensor_scalar(z, z, 1.0, None, ALU.add))
            c(DVE.reciprocal(inh, z))
            c(DVE.tensor_scalar(z, inh, CENTER, None, ALU.subtract))
            c(DVE.tensor_scalar(w, z, -1.0, None, ALU.mult))
            v = c(DVE.tensor_tensor(z, z, w, ALU.max))
            need(SCL, v)
            ac.mark(SCL.activation(w, z, ACT.Exp, scale=-10.0))
            v = ac.mark(SCL.activation(fb, z, ACT.Exp, scale=-1.0 / 0.3))
            need(DVE, v)
            c(DVE.tensor_scalar(z, inh, LOWER, None, ALU.is_ge))
            c(DVE.tensor_tensor(w, w, z, ALU.mult))
            c(DVE.tensor_scalar(z, inh, UPPER, None, ALU.is_le))
            c(DVE.tensor_tensor(w, w, z, ALU.mult))
            c(DVE.tensor_reduce(out=red["a"][:, :], in_=w, axis=AX, op=ALU.add))
            c(DVE.tensor_scalar(red["a"][:, :], red["a"][:, :], 1e-8, None, ALU.is_lt))
            c(DVE.tensor_scalar(red["b"][:, :], red["a"][:, :], -1.0, 1.0, ALU.mult, ALU.add))
            top_mask(dv, r["d"], E, 2, r["a"], r["b"])
            c(DVE.tensor_tensor(fb, fb, z, ALU.mult))
            c(DVE.tensor_reduce(out=red["c"][:, :], in_=fb, axis=AX, op=ALU.add))
            c(DVE.tensor_scalar(red["c"][:, :], red["c"][:, :], 1e-8, None, ALU.max))
            c(DVE.reciprocal(red["c"][:, :], red["c"][:, :]))
            c(DVE.tensor_tensor(red["c"][:, :], red["c"][:, :], red["a"][:, :], ALU.mult))
            c(DVE.tensor_tensor(fb, fb, bcast(red["c"][:, :], E), ALU.mult))
            c(DVE.tensor_tensor(w, w, bcast(red["b"][:, :], E), ALU.mult))
            c(DVE.tensor_tensor(w, w, fb, ALU.add))
            c(DVE.tensor_reduce(out=red["c"][:, :], in_=w, axis=AX, op=ALU.add))
            c(DVE.tensor_scalar(red["c"][:, :], red["c"][:, :], 1e-8, None, ALU.max))
            c(DVE.reciprocal(red["c"][:, :], red["c"][:, :]))
            c(DVE.tensor_scalar(red["c"][:, :], red["c"][:, :], 0.5, None, ALU.mult))
            v = c(DVE.tensor_tensor(wtab[:, :, 0:E], w, bcast(red["c"][:, :], E), ALU.mult))
            return expert_loop(E, a["ffn0_w"], tag, v)

        def ffn1(tag, updated):
            E = 32
            xT = layernorm_T(updated)
            dv, ac = track(f"route_dve"), track(f"route_act")
            lg = logits(Wr1, E, xT, tag)
            z, w, sc = (r[n][:, :, :] for n in "abd")
            ps = bank[2][:, 0:NT * E].rearrange("p (t e) -> p t e", e=E)
            need(DVE, lg)
            c = lambda ins: chained(dv, DVE, ins)
            c(DVE.tensor_tensor(z, ps, rbias[:, :].unsqueeze(1).broadcast_to([P, NT, E]), ALU.add))
            c(DVE.tensor_reduce(out=red["a"][:, :], in_=z, axis=AX, op=ALU.max))
            v = c(DVE.tensor_tensor(z, z, bcast(red["a"][:, :], E), ALU.subtract))
            need(SCL, v)
            v = ac.mark(SCL.activation(z, z, ACT.Exp))
            need(DVE, v)
            c(DVE.tensor_reduce(out=red["a"][:, :], in_=z, axis=AX, op=ALU.add))
            c(DVE.reciprocal(red["a"][:, :], red["a"][:, :]))
            c(DVE.tensor_tensor(sc, z, bcast(red["a"][:, :], E), ALU.mult))
            top_mask(dv, r["d"], E, 4, r["a"], r["b"])
            c(DVE.tensor_tensor(sc, sc, z, ALU.mult))
            c(DVE.tensor_reduce(out=red["a"][:, :], in_=sc, axis=AX, op=ALU.add))
            c(DVE.tensor_scalar(red["a"][:, :], red["a"][:, :], 1e-12, None, ALU.max))
            c(DVE.reciprocal(red["a"][:, :], red["a"][:, :]))
            c(DVE.tensor_scalar(red["a"][:, :], red["a"][:, :], 0.5, None, ALU.mult))
            c(DVE.tensor_tensor(wtab[:, :, 0:E], sc, bcast(red["a"][:, :], E), ALU.mult))
            v = c(DVE.memset(wtab[:, :, E:E + 4], 0.5))
            return expert_loop(E + 4, a["ffn1_w"], tag, v)

        H, HD, M = 16, 8, 64
        NK = H // 2
        R = S // M
        qT, kT = sb("qT", [P, T]), sb("kT", [P, T])
        v_sb = sb("v_sb", [P, NT, D])
        klm, qlm = sb("klm", [P, B, M]), sb("qlm", [P, B, M])
        QB, KB = sb("QB", [P, B, H * M]), sb("KB", [P, B, H * M])
        m1 = [sb(f"m1_{p}", [P, NK]) for p in range(2)]
        r1 = sb("r1", [P, NK, 2])
        E3, E3T = sg, hT
        m3, s3 = sb("m3", [P, B, NK]), sb("s3", [P, B, NK])
        m2, s2, rden = sb("m2", [P, NK]), sb("s2", [P, NK]), sb("rden", [P, B, NK])
        Kc = [sb(f"Kc{b}", [P, NK, M]) for b in range(2)]
        KTbd, KTc = sb("KTbd", [P, NK, P]), sb("KTc", [P, NK, M])
        Kbd, Abd, Pbd = ([sb(f"{n}{b}", [P, NK, P]) for b in range(B)] for n in ("Kbd", "Abd", "Pbd"))
        E1 = [Abd[2 + p][:, :, :].rearrange("p k m -> p (k m)") for p in range(2)]
        E1T = [Pbd[p] for p in range(2)]
        Tc = [sb(f"Tc{b}", [P, NK, M]) for b in range(B)]
        Ac = sb("Ac", [P, NK, M])
        y = sb("y", [P, B, NK, HD])
        WC = 2 * HD + 2
        WB = sb("WB", [P, B, NK, WC])
        sv = [sb(f"sv{p}", [P, D]) for p in range(2)]
        svT = [sb(f"svT{p}", [P, D]) for p in range(2)]
        I7, I15, I13 = sb("I7", [P, M]), sb("I15", [P, M]), sb("I13", [P, M])
        pe, dv, ac, po = track("attn_pe"), track("attn_dve"), track("attn_act"), track("attn_pool")
        newton = [{n: track(f"newton{b}_{n}") for n in ("pe", "dve", "act", "y")} for b in range(B)]

        def V(ins):
            return chained(dv, DVE, ins)

        def m8(ap2):
            return ap2.unsqueeze(2).broadcast_to([P, NK, M])

        def pv(b):
            return b[:, :].rearrange("p (k m) -> p k m", m=M)

        def pairs(ap2):
            return ap2.unsqueeze(1).broadcast_to([P, NK, M])

        def attn0_constants():
            for b in range(B):
                for t in (Kbd[b], Abd[b], Pbd[b]):
                    chained(po, POOL, POOL.memset(t[:, :, :], 0.0))
            chained(po, POOL, POOL.memset(WB[:, :, :, :], 0.0))
            need(POOL, po.now())
            chained(po, POOL, POOL.memset(WB[0:64, :, :, 2 * HD:2 * HD + 1], 1.0))
            v = chained(po, POOL, POOL.memset(WB[64:P, :, :, 2 * HD + 1:WC], 1.0))
            for t, f in ((I7, 7.0), (I15, 15.0), (I13, 3.25)):
                dv.mark(DVE.tensor_scalar(t[:, :], ident2[:, :], f, None, ALU.mult))
            need(DVE, dv.now(), v)
            need(SCL, dv.now(), v)
            need(PE, dv.now(), v)

        def attn0(updated):
            xT = layernorm_T(updated)
            for e in (DVE, SCL, PE, POOL):
                need(e, updated[-1])
            q_at, k_at, v_at, QB_at, KB_at, klm_at, proj = ([None] * B for _ in range(7))
            free = {}

            def project(b):
                cols = slice(b * S, (b + 1) * S)
                bq, bk, bv = bank[3 * (b % 2)], bank[3 * (b % 2) + 1], bank[3 * (b % 2) + 2]
                need(PE, xT[b], *free.get(b - 2, ()))
                pq = pe.mark(PE.matmul(bq[:, :], wqkv[:, 0:D], xnT[:, cols], start=True, stop=True))
                pk = pe.mark(PE.matmul(bk[:, :], wqkv[:, D:2 * D], xnT[:, cols], start=True, stop=True))
                for j in range(TB):
                    t = b * TB + j
                    last = PE.matmul(bv[:, j * P:(j + 1) * P], xnT[:, t * P:(t + 1) * P], wqkv[:, 2 * D:3 * D],
                                     start=True, stop=True)
                pvv = pe.mark(last)
                need(SCL, pq)
                q_at[b] = ac.mark(SCL.mul(qT[:, cols], bq[:, :], HD ** -0.5))
                need(DVE, pk)
                k_at[b] = dv.mark(DVE.tensor_copy(kT[:, cols], bk[:, :]))
                need(SCL, pvv)
                v_at[b] = ac.mark(SCL.copy(v_sb[:, b * TB:(b + 1) * TB, :], bv[:, :].rearrange("p (j d) -> p j d", d=D)))
                free[b] = (q_at[b], k_at[b], v_at[b])

            def landmarks(b):
                cols = slice(b * S, (b + 1) * S)
                need(DVE, q_at[b], k_at[b])
                for src, lm in ((qT, qlm), (kT, klm)):
                    dv.mark(DVE.tensor_reduce(out=lm[:, b, :], in_=src[:, cols].rearrange("p (m r) -> p m r", r=R), axis=AX, op=ALU.add))
                need(DVE, dv.now())
                for lm in (qlm, klm):
                    klm_at[b] = dv.mark(DVE.tensor_scalar(lm[:, b, :], lm[:, b, :], 1.0 / R, None, ALU.mult))
                need(DVE, dv.now())
                need(POOL, dv.now())
                hm = headmask[:, :].unsqueeze(2).broadcast_to([P, H, M])
                for eng, tr, lm, dst, at in ((DVE, dv, qlm, QB, QB_at), (POOL, po, klm, KB, KB_at)):
                    at[b] = chained(tr, eng, eng.tensor_tensor(dst[:, b, :].rearrange("p (h m) -> p h m", m=M),
                                                      lm[:, b, :].unsqueeze(1).broadcast_to([P, H, M]), hm, ALU.mult))

            skew(B, project, landmarks)

            Qp = lambda b, k: QB[:, b, k * 2 * M:(k + 1) * 2 * M]
            e3_at, e3T_free, s_free, t_free, sc_at, tr_at, kv_done = {}, {}, {}, {}, {}, {}, {}
            bankK, bank2 = bank[4], bank[5]
            fronts = (q_at[-1], k_at[-1], v_at[-1])

            def scores3(i):
                b, k = divmod(i, NK)
                need(PE, QB_at[b], k_at[b], s_free.get(i - 2, fronts[0]), fronts[1], fronts[2])
                sc_at[i] = pe.mark(PE.matmul(bank[i % 2][:, :], Qp(b, k), kT[:, b * S:(b + 1) * S], start=True, stop=True))
                need(DVE, sc_at[i])
                v = dv.mark(DVE.tensor_reduce(out=m3[:, b, k:k + 1], in_=bank[i % 2][:, :], axis=AX, op=ALU.max, negate=True))
                need(SCL, v, tr_at.get(i - 2, (None, 0)))
                e3_at[i] = s_free[i] = ac.mark(SCL.activation(E3[i % 2][:, :], bank[i % 2][:, :], ACT.Exp,
                                                              bias=m3[:, b, k:k + 1], accum_out=s3[:, b, k:k + 1]))

            def transpose3(i):
                b, k = divmod(i, NK)
                bt = bank[2 + i % 2]
                need(PE, e3_at[i], t_free.get(i - 2, (None, 0)))
                for j in range(TB):
                    last = PE.transpose(bt[:, j * P:(j + 1) * P], E3[i % 2][:, j * P:(j + 1) * P], ident[:, :])
                tr_at[i] = pe.mark(last)
                eng, tr = ((SCL, ac), (DVE, dv))[i % 2]
                need(eng, tr_at[i], kv_done.get(i - 2, (None, 0)))
                cp = SCL.copy(E3T[i % 2][:, :], bt[:, :]) if eng is SCL else DVE.tensor_copy(E3T[i % 2][:, :], bt[:, :])
                t_free[i] = tr.mark(cp)

            def values3(i):
                b, k = divmod(i, NK)
                need(PE, t_free[i])
                for j in range(TB):
                    last = PE.matmul(bankK[:, (b * NK + k) * 16:(b * NK + k + 1) * 16], E3T[i % 2][:, j * P:(j + 1) * P],
                                     v_sb[:, b * TB + j, k * 16:(k + 1) * 16], start=(j == 0), stop=(j == TB - 1))
                kv_done[i] = pe.mark(last)

            k2 = {}

            def kernel2(i):
                b, step = divmod(i, NK)
                kc = Kc[b % 2]
                if step == 0:
                    need(PE, k2.get("free2", fronts[2]), klm_at[b])
                    for k in range(NK):
                        last = PE.matmul(bank2[:, k * M:(k + 1) * M], Qp(b, k), klm[:, b, :], start=True, stop=True)
                    need(DVE, pe.mark(last), k2.get("bd", (None, 0)))
                    V(DVE.tensor_reduce(out=m2[:, :], in_=pv(bank2), axis=AX, op=ALU.max))
                    k2["sub"] = dv.mark(DVE.tensor_tensor(kc[:, :, :], pv(bank2), m8(m2[:, :]), ALU.subtract))
                elif step == 1:
                    need(SCL, k2["sub"])
                    k2["exp"] = ac.mark(SCL.activation(kc[:, :, :], kc[:, :, :], ACT.Exp))
                elif step == 2:
                    need(DVE, k2["exp"])
                    V(DVE.tensor_reduce(out=s2[:, :], in_=kc[:, :, :], axis=AX, op=ALU.add))
                    V(DVE.reciprocal(s2[:, :], s2[:, :]))
                    k2["K"] = dv.mark(DVE.tensor_tensor(kc[:, :, :], kc[:, :, :], m8(s2[:, :]), ALU.mult))
                    need(POOL, k2["K"])
                    chained(po, POOL, POOL.tensor_copy(Kbd[b][0:64, :, 0:M], kc[0:64]))
                    k2["bd"] = chained(po, POOL, POOL.tensor_copy(Kbd[b][64:P, :, M:P], kc[64:P]))
                elif step == 4:
                    need(PE, k2["K"], k2["bd"], k2["sub"], k2.get("ktfree", (None, 0)))
                    k2["sum"] = pe.mark(PE.matmul(bank2[:, :], blockones[:, :], kc[:, :, :], start=True, stop=True))
                    for k in range(NK):
                        last = PE.transpose(bank[6 + k // 4][:, k % 4 * P:(k % 4 + 1) * P], Kbd[b][:, k, :], ident[:, :])
                    k2["kt"] = pe.mark(last)
                    need(DVE, k2["sum"])
                    V(DVE.tensor_reduce(out=rden[:, b, :], in_=pv(bank2), axis=AX, op=ALU.max))
                    k2["rden"] = V(DVE.reciprocal(rden[:, b, :], rden[:, b, :]))
                    need(SCL, k2["kt"], k2.get("afree", (None, 0)))
                    for h in range(2):
                        k2["ktbd"] = k2["ktfree"] = ac.mark(SCL.copy(KTbd[:, 4 * h:4 * h + 4, :],
                                                                     bank[6 + h][:, :].rearrange("p (k m) -> p k m", m=P)))
                elif step == 5:
                    need(POOL, k2["ktbd"])
                    chained(po, POOL, POOL.tensor_copy(KTc[0:64, :, :], KTbd[0:64, :, 0:M]))
                    k2["ktc"] = chained(po, POOL, POOL.tensor_copy(KTc[64:P, :, :], KTbd[64:P, :, M:P]))
                elif step == 7:
                    need(PE, k2["ktc"], k2["rden"])
                    for k in range(NK):
                        last = PE.matmul(bank2[:, k * M:(k + 1) * M], KTbd[:, k, :], KTc[:, k, :], start=True, stop=True)
                    k2["afree"] = pe.mark(last)
                    need(DVE, k2["afree"], k2.get("Abd", (None, 0)))
                    k2["free2"] = V(DVE.tensor_tensor(Ac[:, :, :], pv(bank2), m8(rden[:, b, :]), ALU.mult))
                    need(POOL, k2["free2"])
                    chained(po, POOL, POOL.tensor_copy(Abd[b][0:64, :, 0:M], Ac[0:64]))
                    k2["Abd"] = chained(po, POOL, POOL.tensor_copy(Abd[b][64:P, :, M:P], Ac[64:P]))
                    V(DVE.scalar_tensor_tensor(out=Tc[b][:, :, :], in0=Ac[:, :, :], scalar=-1.0, in1=pairs(I7[:, :]),
                                               op0=ALU.mult, op1=ALU.add))

            skew(B * NK, scores3, transpose3, values3, kernel2)
            need(DVE, kv_done[B * NK - 1], ac.now())
            V(DVE.reciprocal(s3[:, :, :], s3[:, :, :]))
            kv = bankK[:, :].rearrange("p (g d) -> p g d", d=2 * HD)
            for h in range(2):
                rows = slice(64 * h, 64 * h + 64)
                y_at = V(DVE.tensor_tensor(y[rows, :, :, :].rearrange("p b k d -> p (b k) d"), kv[rows, :, HD * h:HD * h + HD],
                                           s3[rows, :, :].rearrange("p b k -> p (b k)").unsqueeze(2).broadcast_to([64, B * NK, HD]), ALU.mult))

            need(PE, y_at, k2["Abd"], dv.now())
            need(SCL, y_at, k2["Abd"])
            need(DVE, k2["Abd"])

            def newton_step(last_step):
                pe_ = [n["pe"] for n in newton]
                for b in range(B):
                    n = newton[b]
                    need(PE, n["dve"].now(), n["act"].now())
                for c, diag in ((-1.0, I15), (-0.25, I13)):
                    for b in range(B):
                        n = newton[b]
                        need(PE, n["dve"].now())
                        for k in range(NK):
                            last = PE.matmul(bank[b][:, k * M:(k + 1) * M], Abd[b][:, k, :], Tc[b][:, k, :], start=True, stop=True)
                        need(DVE, n["pe"].mark(last))
                        n["dve"].mark(DVE.scalar_tensor_tensor(out=Tc[b][:, :, :], in0=pv(bank[b]), scalar=c, in1=pairs(diag[:, :]),
                                                               op0=ALU.mult, op1=ALU.add))
                        if diag is I13:
                            need(SCL, n["dve"].now(), n["y"].now())
                            SCL.copy(Pbd[b][0:64, :, 0:M], Tc[b][0:64])
                            n["act"].mark(SCL.copy(Pbd[b][64:P, :, M:P], Tc[b][64:P]))
                for b in range(B):
                    n = newton[b]
                    if not last_step:
                        need(PE, n["dve"].now())
                        for k in range(NK):
                            last = PE.matmul(bank[b][:, k * M:(k + 1) * M], Abd[b][:, k, :], Tc[b][:, k, :], start=True, stop=True)
                        at = n["pe"].mark(last)
                        need(DVE, at, n["act"].now())
                        n["dve"].mark(DVE.scalar_tensor_tensor(out=Tc[b][:, :, :], in0=pv(bank[b]), scalar=-1.0, in1=pairs(I7[:, :]),
                                                               op0=ALU.mult, op1=ALU.add))
                    need(PE, n["act"].now())
                    for k in range(NK):
                        last = PE.matmul(bank[4 + b][:, k * HD:(k + 1) * HD], Pbd[b][:, k, :], y[:, b, k, :], start=True, stop=True)
                    n["y"].mark(last)
                    need(SCL, n["y"].now())
                    ymark = SCL.copy(y[:, b, :, :], bank[4 + b][:, 0:NK * HD].rearrange("p (k d) -> p k d", d=HD))
                    if not last_step:
                        need(SCL, n["dve"].now())
                        SCL.copy(Abd[b][0:64, :, 0:M], pv(bank[b])[0:64])
                        n["act"].mark(SCL.copy(Abd[b][64:P, :, M:P], pv(bank[b])[64:P]))
                    else:
                        n["act"].mark(ymark)

            marks = {t: c for n in newton for t, c in ((n["pe"], 3), (n["dve"], 3), (n["act"], 2), (n["y"], 1))}
            with loop(nc, 5, marks):
                newton_step(False)
            newton_step(True)

            for b in range(B):
                need(PE, newton[b]["act"].now())
                for k in range(NK):
                    last = PE.matmul(bank[4 + b][:, k * HD:(k + 1) * HD], Kbd[b][:, k, :], y[:, b, k, :], start=True, stop=True)
                need(DVE, pe.mark(last))
                kv = bank[4 + b][:, 0:NK * HD].rearrange("p (k d) -> p k d", d=HD)
                for h in range(2):
                    rows = slice(64 * h, 64 * h + 64)
                    WB_at = dv.mark(DVE.tensor_tensor(WB[rows, b, :, HD * h:HD * h + HD], kv[rows, :, :],
                                                      rden[rows, b, :].unsqueeze(2).broadcast_to([64, NK, HD]), ALU.mult))
            need(PE, dv.now(), *(n["dve"].now() for n in newton))

            e1_at, h_free, c_done, t1_free, sv_done, sv_free, svT_done, svT_ev, pr_done = ({} for _ in range(9))

            def scores1(t):
                b, j = divmod(t, TB)
                need(PE, KB_at[b], q_at[b])
                for h in range(2):
                    i = 2 * t + h
                    need(PE, h_free.get(i - 3, (None, 0)))
                    at = pe.mark(PE.matmul(bank[i % 3][:, :], qT[:, t * P:(t + 1) * P], KB[:, b, h * 512:(h + 1) * 512], start=True, stop=True))
                    need(DVE, at, c_done.get(t - 2, (None, 0)))
                    V(DVE.tensor_reduce(out=m1[h][:, :], in_=pv(bank[i % 3]), axis=AX, op=ALU.max))
                    h_free[i] = dv.mark(DVE.tensor_tensor(E1[t % 2][:, h * 512:(h + 1) * 512].rearrange("p (k m) -> p k m", m=M),
                                                          pv(bank[i % 3]), m8(m1[h][:, :]), ALU.subtract))
                    need(SCL, h_free[i])
                    e1_at[t] = ac.mark(SCL.activation(E1[t % 2][:, h * 512:(h + 1) * 512], E1[t % 2][:, h * 512:(h + 1) * 512], ACT.Exp))

            def transpose1(t):
                need(PE, e1_at[t])
                for h in range(2):
                    need(PE, t1_free.get((t - 1, h), (None, 0)))
                    for k in range(4):
                        last = PE.transpose(bank[3 + h][:, k * P:(k + 1) * P], E1[t % 2][:, (4 * h + k) * P:(4 * h + k + 1) * P], ident[:, :])
                    c_done[t] = pe.mark(last)
                    need(SCL, c_done[t], sv_done.get(t - 2, (None, 0)))
                    t1_free[t, h] = ac.mark(SCL.copy(E1T[t % 2][:, 4 * h:4 * h + 4, :], bank[3 + h][:, :].rearrange("p (k t) -> p k t", t=P)))

            def values1(t):
                b = t // TB
                need(PE, t1_free[t, 1], sv_free.get(t - 1, (None, 0)))
                for k in range(NK):
                    last = PE.matmul(bank[5][:, k * WC:(k + 1) * WC], E1T[t % 2][:, k, :], WB[:, b, k, :], start=True, stop=True)
                sv_done[t] = pe.mark(last)
                o = bank[5][:, 0:NK * WC].rearrange("p (k c) -> p k c", c=WC)
                need(DVE, sv_done[t], svT_done.get(t - 2, (None, 0)))
                V(DVE.reciprocal(r1[:, :, :], o[:, :, 2 * HD:WC]))
                sv_free[t] = dv.mark(DVE.tensor_tensor(sv[t % 2][:, :].rearrange("p (k h d) -> p k h d", h=2, d=HD),
                                                       o[:, :, 0:2 * HD].rearrange("p k (h d) -> p k h d", d=HD),
                                                       r1[:, :, :].unsqueeze(3).broadcast_to([P, NK, 2, HD]), ALU.mult))

            def transpose_sv(t):
                need(PE, sv_free[t], svT_ev.get(t - 1, (None, 0)))
                svT_done[t] = pe.mark(PE.transpose(bank[6][:, 0:P], sv[t % 2][:, :], ident[:, :]))
                need(SCL, svT_done[t], pr_done.get(t - 2, (None, 0)))
                svT_ev[t] = ac.mark(SCL.copy(svT[t % 2][:, :], bank[6][:, 0:P]))

            res = {}

            def output(t):
                need(PE, svT_ev[t], res.get(t - 1, (None, 0)))
                pr_done[t] = pe.mark(PE.matmul(bank[7][:, 0:D], svT[t % 2][:, :], wproj[:, :], start=True, stop=True))
                need(DVE, pr_done[t])
                res[t] = s_res.mark(DVE.tensor_tensor(x[:, t, :], bank[7][:, 0:D], x[:, t, :], ALU.add))

            skew(NT, scores1, transpose1, values1, transpose_sv, output)
            return [res[TB * b + TB - 1] for b in range(B)]

        NW = 2 * S // P - 1
        Ew = [sb(f"Ew{p}", [P, P]) for p in range(3)]
        EwT = [sb(f"EwT{p}", [P, P]) for p in range(2)]
        mw, sw = sb("mw", [P, B * NW]), sb("sw", [P, B * NW])
        bqs = sb("bqs", [P, 1])
        oT = [sb(f"oT{p}", [P, S]) for p in range(2)]
        ORDER = [w for w in range(0, NW, 2)] + [w for w in range(1, NW, 2)]

        def attn1(updated):
            SC = 1.0 / math.sqrt(8.0)
            xT = layernorm_T(updated)
            for e in (DVE, SCL, PE, POOL):
                need(e, updated[-1])
            vw = QB
            V(DVE.tensor_scalar(bqs[:, :], bq1[:, :], SC, None, ALU.mult))
            need(SCL, dv.now())
            q_at, k_at, v_at = ([None] * B for _ in range(3))

            def project(b):
                cols = slice(b * S, (b + 1) * S)
                need(PE, xT[b])
                if b:
                    need(PE, q_at[b - 1], k_at[b - 1])
                pq = pe.mark(PE.matmul(bank[0][:, :], wq1[:, :], xnT[:, cols], start=True, stop=True))
                pk = pe.mark(PE.matmul(bank[1][:, :], wk1[:, :], xnT[:, cols], start=True, stop=True))
                need(SCL, pq)
                q_at[b] = ac.mark(SCL.activation(qT[:, cols], bank[0][:, :], ACT.Identity, bias=bqs[:, 0:1], scale=SC))
                need(SCL, pk)
                k_at[b] = ac.mark(SCL.activation(kT[:, cols], bank[1][:, :], ACT.Identity, bias=bk1[:, 0:1]))
                for g, n in ((0, 4), (1, NW - 4)):
                    bk = bank[2 + 2 * (b % 2) + g]
                    if b > 1:
                        need(PE, v_at[b - 2])
                    for w in range(n):
                        c = b * S + (4 * g + w) * 64
                        last = PE.matmul(bk[:, w * P:(w + 1) * P], xnT[:, c:c + P], wv1[:, :], start=True, stop=True)
                    need(DVE, pe.mark(last))
                    v_at[b] = dv.mark(DVE.tensor_tensor(vw[:, b, 4 * g * D:(4 * g + n) * D].rearrange("p (w d) -> p w d", d=D),
                                                        bk[:, 0:n * P].rearrange("p (w d) -> p w d", d=D),
                                                        bv1[:, :].unsqueeze(1).broadcast_to([P, n, D]), ALU.add))

            for b in range(B):
                project(b)
            need(PE, dv.now(), ac.now())
            s_at, n_at, t_at, c_at, o_at, res = ({} for _ in range(6))

            def scores(i):
                b, n = divmod(i, NW)
                w = ORDER[n]
                win = slice(b * S + w * 64, b * S + w * 64 + P)
                bs, e = bank[i % 2], Ew[i % 3]
                need(PE, s_at.get(i - 2, (None, 0)))
                need(DVE, pe.mark(PE.matmul(bs[:, 0:P], qT[:, win], kT[:, win], start=True, stop=True)))
                v = dv.mark(DVE.tensor_reduce(out=mw[:, i:i + 1], in_=bs[:, 0:P], axis=AX, op=ALU.max, negate=True))
                need(SCL, v, t_at.get(i - 3, (None, 0)))
                s_at[i] = ac.mark(SCL.activation(e[:, :], bs[:, 0:P], ACT.Exp, bias=mw[:, i:i + 1], accum_out=sw[:, i:i + 1]))

            def normalise(i):
                e = Ew[i % 3]
                need(DVE, s_at[i])
                V(DVE.reciprocal(sw[:, i:i + 1], sw[:, i:i + 1]))
                n_at[i] = dv.mark(DVE.tensor_scalar(e[:, :], e[:, :], sw[:, i:i + 1], None, ALU.mult))

            def transposed(i):
                need(PE, n_at[i], c_at.get(i - 2, (None, 0)))
                t_at[i] = pe.mark(PE.transpose(bank[2 + i % 2][:, 0:P], Ew[i % 3][:, :], ident[:, :]))
                need(SCL, t_at[i], o_at.get(i - 2, (None, 0)))
                c_at[i] = ac.mark(SCL.copy(EwT[i % 2][:, :], bank[2 + i % 2][:, 0:P]))

            ev = {}

            def values(i):
                b, n = divmod(i, NW)
                w = ORDER[n]
                bo = bank[4 + b % 2]
                need(PE, c_at[i], ev.get(b - 2, (None, 0)))
                o_at[i] = pe.mark(PE.matmul(bo[:, w * 64:w * 64 + P], vw[:, b, w * D:(w + 1) * D], EwT[i % 2][:, :],
                                            start=(n == 0), stop=(n == NW - 1), skip_group_check=True))
                if n == NW - 1:
                    need(SCL, o_at[i], res.get(b - 2, (None, 0)))
                    o = oT[b % 2]
                    SCL.copy(o[:, 0:64], bo[:, 0:64])
                    SCL.mul(o[:, 64:S - 64], bo[:, 64:S - 64], 0.5)
                    ev[b] = ac.mark(SCL.copy(o[:, S - 64:S], bo[:, S - 64:S]))

            def output(i):
                b, n = divmod(i, NW)
                if n != NW - 1:
                    return
                bo = bank[6 + b % 2]
                need(PE, ev[b], res.get(b - 2, (None, 0)))
                for j in range(TB):
                    last = PE.matmul(bo[:, j * P:(j + 1) * P], oT[b % 2][:, j * P:(j + 1) * P], wo1[:, :], start=True, stop=True)
                need(DVE, pe.mark(last))
                xs = x[:, b * TB:(b + 1) * TB, :]
                V(DVE.tensor_tensor(xs, bo[:, :].rearrange("p (j d) -> p j d", d=D), xs, ALU.add))
                res[b] = s_res.mark(DVE.tensor_tensor(xs, xs, bo1[:, :].unsqueeze(1).broadcast_to([P, TB, D]), ALU.add))

            skew(B * NW, scores, normalise, transposed, values, output)
            return [res[b] for b in range(B)]

        attn0_constants()
        up = [s_x.now()] * NG
        up = ffn0("f0a", up)
        up = attn0(up)
        up = ffn0("f0b", up)
        up = ffn1("f1a", up)
        up = attn1(up)
        up = ffn1("f1b", up)
        s_out = track("stored", 16)
        need(SP, s_res.now())
        s_out.mark(SP.dma_start(out.rearrange("b (t p) d -> p (b t) d", p=P), x[:, :, :]))
        need(SP, s_out.now())


LOOP_TRACKS = ("expert_load0 expert_load1 expert_gate expert_up expert_down expert_silu expert_hidden x_updated "
               + " ".join(f"newton{b}_{n}" for b in range(4) for n in ("pe", "dve", "act", "y"))).split()

_X = "x wqkv wproj Wr temp WrT rbias Wq Wk Wv Wo bq bk bv bo ffn0_w ffn1_w".split()


def kernel(**inputs):
    import numpy as _np
    import concourse.bacc as _bacc
    from concourse import mybir as _mybir
    from concourse.bass_utils import run_bass_kernel_spmd as _run

    i = {k: _np.asarray(v) for k, v in inputs.items()}
    t = lambda w: w.transpose(0, 2, 1)
    rows = lambda w: w.reshape(4, P, w.shape[1])
    g0, u0, d0 = (i[f"L0_ffn_{n}"] for n in ("Wg", "Wu", "Wd"))
    g1 = _np.concatenate([t(i["L1_ffn_gate_w"]), t(rows(i["L1_ffn_sgate_w"]))])
    u1 = _np.concatenate([t(i["L1_ffn_up_w"]), t(rows(i["L1_ffn_sup_w"]))])
    d1 = _np.concatenate([t(i["L1_ffn_down_w"]), i["L1_ffn_sdown_w"].T.reshape(4, P, P)])
    a = {
        "x": i["L0_attn_x"], "wqkv": i["L0_attn_w_qkv"], "wproj": i["L0_attn_w_proj"],
        "Wr": i["L0_ffn_Wr"], "temp": i["L0_ffn_temperature"],
        "WrT": i["L1_ffn_router_w"].T, "rbias": i["L1_ffn_router_bias"],
        "Wq": i["L1_attn_Wq"], "Wk": i["L1_attn_Wk"], "Wv": i["L1_attn_Wv"], "Wo": i["L1_attn_Wo"],
        "bq": i["L1_attn_bq"], "bk": i["L1_attn_bk"], "bv": i["L1_attn_bv"], "bo": i["L1_attn_bo"],
        "ffn0_w": _np.stack([g0, u0, d0], axis=2),
        "ffn1_w": _np.stack([g1, u1, d1], axis=2),
    }
    nc = _bacc.Bacc("TRN2", target_bir_lowering=False, num_devices=1)
    arrays, aps = {}, {}
    for name in _X:
        v = _np.ascontiguousarray(a[name])
        arrays[f"in_{name}"] = v
        aps[name] = nc.dram_tensor(f"in_{name}", v.shape, _mybir.dt.from_np(v.dtype), kind="ExternalInput").ap()
    out = nc.dram_tensor("out", a["x"].shape, _mybir.dt.float32, kind="ExternalOutput").ap()
    build(nc, aps, out)
    return _run(nc, [arrays], core_ids=[0]).results[0]["out"]
```

```python
import math
from contextlib import ExitStack, contextmanager

import numpy as np
import concourse.bass as bass
from concourse import mybir

F32 = mybir.dt.float32
F32R = mybir.dt.float32r
U32 = mybir.dt.uint32
ALU = mybir.AluOpType
ACT = mybir.ActivationFunctionType
AX = mybir.AxisListType.X
P = 128


class Track:

    def __init__(self, sem, step=1):
        self.sem, self.step = sem, step
        self.base, self.local, self.per_iter, self.i = 0, 0, None, None

    def now(self):
        if self.i is None:
            return self.sem, self.base + self.local
        return self.sem, self.i * self.per_iter + (self.base + self.local)

    def mark(self, instruction):
        instruction.then_inc(self.sem, self.step)
        self.local += self.step
        return self.now()


def need(engine, *values):
    for sem, value in values:
        if sem is not None and not (isinstance(value, int) and value <= 0):
            engine.wait_ge(sem, value)


def skew(n, *stages):
    for t in range(n + len(stages) - 1):
        for k, stage in enumerate(stages):
            if 0 <= t - k < n:
                stage(t - k)


@contextmanager
def loop(nc, count, marks):
    with nc.Fori(0, count) as i:
        for t, n in marks.items():
            t.base, t.local, t.per_iter, t.i = t.base + t.local, 0, n * t.step, i
        yield i
        wrong = {t.sem.name: t.local // t.step for t, n in marks.items() if t.local != n * t.step}
        assert not wrong, f"marks per iteration: {wrong}"
        for t in marks:
            t.base, t.local, t.i = t.base + count * t.per_iter, 0, None


def build(nc, a, out):
    B, S, D = a["x"].shape
    T = B * S
    NT = T // P
    TB = S // P
    GW = 4 * P
    NG = T // GW
    PE, DVE, SCL, POOL, SP = nc.tensor, nc.vector, nc.scalar, nc.gpsimd, nc.sync

    with ExitStack() as ctx:
        tracks = {}

        def sb(name, shape, dt=F32):
            return ctx.enter_context(nc.sbuf_tensor(name, shape, dt))

        def track(name, step=1):
            if name not in tracks:
                tracks[name] = Track(ctx.enter_context(nc.semaphore(name)), step)
            return tracks[name]

        for name in LOOP_TRACKS:
            t = track(name, 16 if "load" in name else 1)
            SP.sem_inc(t.sem, t.step)
            t.local = t.step
        nc.all_engine_barrier()

        bank = [ctx.enter_context(nc.psum_tensor(f"bank{n}", [P, 512], F32)) for n in range(8)]

        x = sb("x", [P, NT, D])
        xn = sb("xn", [P, NT, D])
        xnT = sb("xnT", [P, T])
        ident = sb("ident", [P, P])
        ident2 = sb("ident2", [P, 64])
        headmask = sb("headmask", [P, 16])
        blockones = sb("blockones", [P, P])
        iota_e = sb("iota_e", [P, 32])
        stats = sb("stats", [P, NT, 6])
        mv = sb("mv", [P, NT, 2])
        rstd = sb("rstd", [P, NT])

        s_x = [track(f"x_loaded{g}", 16) for g in range(NG)]
        s_w = track("small_loaded", 16)
        s_c = track("const_pool")
        s_cv = track("const_dve")

        xr = a["x"].rearrange("b (t p) d -> p (b t) d", p=P)
        for g in range(NG):
            s_x[g].mark(SP.dma_start(x[:, 4 * g:4 * g + 4, :], xr[:, 4 * g:4 * g + 4, :]))

        loaded_x = [t.now() for t in s_x]

        def load(name, shape, src):
            t = sb(name, shape)
            s_w.mark(SCL.dma_start(t[:], src))
            return t

        Wr0 = load("Wr0", [D, 8], a["Wr"])
        temp = load("temp", [P, 1], a["temp"].rearrange("(o a) -> o a", o=1).broadcast_to([P, 1]))
        wqkv = load("wqkv", [D, 3 * D], a["wqkv"])
        wproj = load("wproj", [D, D], a["wproj"])
        Wr1 = load("Wr1", [D, 32], a["WrT"])
        rbias = load("rbias", [P, 32], a["rbias"].rearrange("(o a) -> o a", o=1).broadcast_to([P, 32]))
        wq1, wk1, wv1, wo1 = (load(n, [D, D], a[n]) for n in ("Wq", "Wk", "Wv", "Wo"))
        bq1, bk1 = (load(n, [D, 1], a[n].rearrange("(d o) -> d o", o=1)) for n in ("bq", "bk"))
        bv1, bo1 = (load(n, [P, D], a[n].rearrange("(o d) -> o d", o=1).broadcast_to([P, D])) for n in ("bv", "bo"))

        s_c.mark(POOL.memset(ident[:, :], 0.0))
        s_c.mark(POOL.memset(ident2[:, :], 0.0))
        s_c.mark(POOL.memset(headmask[:, :], 1.0))
        s_c.mark(POOL.iota(iota_e[:, :], pattern=[[1, 32]], base=0, channel_multiplier=0,
                           allow_small_or_imprecise_dtypes=True))
        need(POOL, s_c.now())
        s_c.mark(POOL.affine_select(out=ident[:, :], in_=ident[:, :], compare_op=ALU.not_equal, fill=1.0,
                                    base=0, pattern=[[-1, P]], channel_multiplier=1))
        for base in (0, -64):
            s_c.mark(POOL.affine_select(out=ident2[:, :], in_=ident2[:, :], compare_op=ALU.not_equal, fill=1.0,
                                        base=base, pattern=[[-1, 64]], channel_multiplier=1))
            need(POOL, s_c.now())
        s_c.mark(POOL.affine_select(out=headmask[:, :], in_=headmask[:, :], compare_op=ALU.is_ge, fill=0.0,
                                    base=0, pattern=[[-8, 16]], channel_multiplier=1))
        need(POOL, s_c.now())
        s_c.mark(POOL.affine_select(out=headmask[:, :], in_=headmask[:, :], compare_op=ALU.is_ge, fill=0.0,
                                    base=7, pattern=[[8, 16]], channel_multiplier=-1))
        mhalf = sb("mhalf", [P, NT])
        s_c.mark(POOL.memset(mhalf[:, :], -0.5))
        s_cv.mark(DVE.memset(blockones[0:64, 0:64], 1.0))
        s_cv.mark(DVE.memset(blockones[0:64, 64:P], 0.0))
        s_cv.mark(DVE.memset(blockones[64:P, 0:64], 0.0))
        s_cv.mark(DVE.memset(blockones[64:P, 64:P], 1.0))
        for e in (PE, SCL, DVE):
            need(e, s_c.now(), s_cv.now())
        need(POOL, s_cv.now())

        def small_operands():
            need(SCL, s_w.now())
            need(DVE, s_w.now())
            need(DVE, s_cv.mark(DVE.reciprocal(temp[:, 0:1], temp[:, 0:1])))

        s_res = track("x_updated")

        s_ln = {n: track(f"ln_{n}") for n in ("stats", "pow", "norm", "transposed", "evacuated")}

        def keep_busy(n, b):
            for _ in range(n):
                PE.matmul(b[:, 0:3 * D], ident[:, :], wqkv[:, :], start=True, stop=True)

        def layernorm_T(updated, then=lambda g, xT_at: None, later=lambda g, xT_at: None, banks=(bank[6], bank[7])):
            done, pow_at = [None] * NG, [None] * NG
            warm = updated is not loaded_x
            if warm:
                need(PE, updated[-1])
                keep_busy(5, bank[5])

            def statistics(g):
                ts = range(4 * g, 4 * g + 4)
                need(DVE, updated[g])
                for t in ts:
                    v = s_ln["stats"].mark(DVE.bn_stats(out=stats[:, t, :], in_=x[:, t, :]))
                need(DVE, v)
                for t in ts:
                    v = s_ln["stats"].mark(DVE.bn_aggr(out=mv[:, t, :], in_=stats[:, t, :]))
                need(DVE, v)
                r = rstd[:, 4 * g:4 * g + 4]
                need(POOL, s_ln["stats"].mark(DVE.tensor_scalar(r, mv[:, 4 * g:4 * g + 4, 1], 1e-5, None, ALU.add)))
                pow_at[g] = s_ln["pow"].mark(POOL.tensor_tensor(r, r, mhalf[:, 4 * g:4 * g + 4], ALU.pow))

            def normalise(g):
                need(DVE, pow_at[g])
                if g == 0:
                    need(DVE, s_ln["transposed"].now())
                for t in range(4 * g, 4 * g + 4):
                    v = s_ln["norm"].mark(DVE.tensor_scalar(xn[:, t, :], x[:, t, :], mv[:, t, 0:1], rstd[:, t:t + 1],
                                                            ALU.subtract, ALU.mult))
                b = banks[g % 2]
                need(PE, v, updated[g], done[g - 2] if g > 1 else (None, 0))
                for t in range(4 * g, 4 * g + 4):
                    last = PE.transpose(b[:, t % 4 * P:(t % 4 + 1) * P], xn[:, t, :], ident[:, :])
                need(SCL, s_ln["transposed"].mark(last))
                if g < NG - 1 and warm:
                    keep_busy(2, bank[5])
                done[g] = s_ln["evacuated"].mark(SCL.copy(xnT[:, g * GW:(g + 1) * GW], b[:, :]))

            skew(NG, statistics, normalise, lambda g: then(g, done[g]), lambda g: later(g, done[g]))
            return done

        x_high, x_low = sb("x_high", [P, T], F32R), sb("x_low", [P, T], F32R)
        w_high, w_low = ([sb(f"w_{n}{p}", [P, 2, P], F32R) for p in range(2)] for n in ("high", "low"))
        s_split = track("split")

        s_high = track("x_high_made")

        def split_x(g, xT_at):
            cols = slice(g * GW, (g + 1) * GW)
            need(SCL, xT_at)
            need(POOL, s_high.mark(SCL.copy(x_high[:, cols], xnT[:, cols])))
            return s_split.mark(POOL.tensor_tensor(x_low[:, cols], xnT[:, cols], x_high[:, cols], ALU.subtract))

        wbuf = [sb(f"wbuf{p}", [P, 3, P]) for p in range(2)]
        sg = [sb(f"sg{p}", [P, GW]) for p in range(2)]
        hT = [sb(f"hT{p}", [P, GW]) for p in range(2)]
        wtab = sb("wtab", [P, NT, 32])

        ld = [track(f"expert_load{p}", 16) for p in range(2)]
        ws = [track(f"expert_split{p}") for p in range(2)]
        down = track("expert_down")

        def load(weights, row, p):
            need(SP, down.now())
            ld[p].mark(SP.dma_start(wbuf[p][:, :, :], weights[bass.ds(row, 1), :, :, :]
                                    .rearrange("o p k n -> p (o k) n")))

        def split_w(p):
            need(DVE, ld[p].now())
            need(DVE, ws[p].mark(DVE.tensor_copy(w_high[p][:, :, :], wbuf[p][:, 0:2, :])))
            ws[p].mark(DVE.tensor_tensor(w_low[p][:, :, :], wbuf[p][:, 0:2, :], w_high[p][:, :, :], ALU.subtract))

        NE = 4

        def expert_loop(E, weights, shared, x_at, logits_read, route, route_steps):
            gate, up = track("expert_gate"), track("expert_up")
            silu, hid, acc = track("expert_silu"), track("expert_hidden"), s_res
            psG, psU = bank[0:2], bank[2:4]
            first_row = NE if shared else 0

            def earlier(at, n):
                return at[0], at[1] - n

            def product3(ps, p, n, cols):
                PE.matmul(ps, w_high[p][:, n, :], x_high[:, cols], start=True, stop=False)
                PE.matmul(ps, w_high[p][:, n, :], x_low[:, cols], start=False, stop=False)
                return PE.matmul(ps, w_low[p][:, n, :], x_high[:, cols], start=False, stop=True)

            def gate_up(p, g, q, gate_free, up_free, *inputs):
                cols = slice(g * GW, (g + 1) * GW)
                need(PE, gate_free, *inputs)
                gate.mark(product3(psG[q][:, :], p, 0, cols))
                need(PE, up_free)
                up.mark(product3(psU[q][:, :], p, 1, cols))

            def block(i, shared_block=False, first=False, last=False):
                SI, HI, DN, AC = [silu.now()], [hid.now()], [down.now()], [acc.now()]
                pending, ends = None, []
                psO = bank[4:8] if shared_block else bank[4:6]

                def add(m, g, ps, d):
                    need(DVE, d)
                    xg = x[:, 4 * g:4 * g + 4, :]
                    if shared_block:
                        last_add = DVE.scalar_tensor_tensor(out=xg, in0=ps[:, :].rearrange("p (j d) -> p j d", d=D),
                                                            scalar=0.5, in1=xg, op0=ALU.mult, op1=ALU.add)
                    else:
                        for j in range(4):
                            t = 4 * g + j
                            last_add = DVE.scalar_tensor_tensor(
                                out=x[:, t, :], in0=ps[:, j * P:(j + 1) * P], scalar=wtab[:, t, bass.ds(i * NE + m, 1)],
                                in1=x[:, t, :], op0=ALU.mult, op1=ALU.add)
                    AC.append(acc.mark(last_add))
                    ends.append(AC[-1])

                if first:
                    gate_up(0, 0, 0, (None, 0), (None, 0), x_at[0], ws[0].now())
                for s in range(4 * NE):
                    m, g = divmod(s, 4)
                    p, q = m % 2, s % 2
                    G, U = gate.now(), up.now()
                    if first:
                        for _ in range(route_steps[s]):
                            next(route, None)
                    n = s + 1
                    if not (last and n == 4 * NE):
                        inputs = [ws[n // 4 % 2].now()] if n % 4 == 0 else []
                        if first and n < 4:
                            inputs.append(x_at[n])
                        gate_up(n // 4 % 2, n % 4, n % 2, SI[-1], logits_read if first and n == 1 else HI[-1], *inputs)
                    need(SCL, G, HI[-2] if s else earlier(HI[0], 1))
                    SI.append(silu.mark(SCL.activation(sg[q][:, :], psG[q][:, :], ACT.Silu)))
                    need(DVE, SI[-1], U, DN[-2] if s else earlier(DN[0], 1))
                    HI.append(hid.mark(DVE.tensor_tensor(hT[q][:, :], sg[q][:, :], psU[q][:, :], ALU.mult)))
                    ps = psO[g] if shared_block else psO[q]
                    need(PE, HI[-1])
                    if not shared_block:
                        need(PE, AC[s - 1] if s else earlier(AC[0], 1))
                    for j in range(4):
                        flags = (dict(start=m == j == 0, stop=m == j == NE - 1, skip_group_check=True) if shared_block
                                 else dict(start=True, stop=True))
                        last_product = PE.matmul(ps[:, j * P:(j + 1) * P], hT[q][:, j * P:(j + 1) * P], wbuf[p][:, 2, :], **flags)
                    DN.append(down.mark(last_product))
                    if pending:
                        add(*pending)
                    pending = (m, g, ps, DN[-1]) if not shared_block or m == NE - 1 else None
                    if g == 2 and not (last and m == NE - 1):
                        split_w(1 - p)
                    if g == 3 and not (last and m >= NE - 2):
                        load(weights, (0 if shared_block else i * NE + first_row) + m + 2, p)
                add(*pending)
                return ends[-NG:]

            if shared:
                block(0, shared_block=True, first=True)
            else:
                block(0, first=True)
            for _ in route:
                pass
            done_blocks = 0 if shared else 1
            blocks = E // NE
            per_block = {gate: 16, up: 16, down: 16, silu: 16, hid: 16, acc: 16, ld[0]: 2, ld[1]: 2, ws[0]: 4, ws[1]: 4}
            if blocks - 1 > done_blocks:
                with loop(nc, blocks - 1 - done_blocks, per_block) as i:
                    block(i)
            return block(blocks - 1, last=True)

        r = {n: sb(f"r_{n}", [P, NT, 32]) for n in ("a", "b", "c", "d")}
        top = sb("top", [P, NT, 8])
        topi = sb("topi", [P, NT, 8], U32)
        topf = sb("topf", [P, NT, 8])
        red = {n: sb(f"red_{n}", [P, NT]) for n in ("a", "b", "c", "d")}

        def chained(tr, engine, instruction):
            v = tr.mark(instruction)
            need(engine, v)
            return v

        def routed_layernorm(W, E, updated, weights):
            x_at, lg = [], []

            def group(g, xT_at):
                need(PE, xT_at, updated[-1], s_w.now())
                for t in range(4 * g, 4 * g + 4):
                    last = PE.matmul(bank[3][:, t * E:(t + 1) * E], xnT[:, t * P:(t + 1) * P], W[:, :], start=True, stop=True)
                lg.append(track("route_logits").mark(last))
                if g == NG - 2:
                    split_w(0)

            load(weights, 0, 0)
            load(weights, 1, 1)
            layernorm_T(updated, group, lambda g, xT_at: x_at.append(split_x(g, xT_at)))
            return x_at, lg[-1]

        def bcast(ap2, n):
            return ap2.unsqueeze(2).broadcast_to([P, NT, n])

        ROUTE0 = [24, 100] + [0] * (4 * NE - 2)
        ROUTE1 = [0] + [3] * (4 * NE - 1)

        def top_mask(tr, scores, E, k, mask, tmp):
            for t in range(NT):
                v = tr.mark(DVE.max(out=top[:, t, :], in_=scores[:, t, 0:E]))
                if t % 4 == 3:
                    yield
            need(DVE, v)
            for t in range(NT):
                v = tr.mark(DVE.max_index(out=topi[:, t, :], in_max=top[:, t, :], in_values=scores[:, t, 0:E]))
                if t % 4 == 3:
                    yield
            need(DVE, v)
            chained(tr, DVE, DVE.tensor_copy(topf[:, :, :], topi[:, :, :]))
            yield
            io = iota_e[:, 0:E].unsqueeze(1).broadcast_to([P, NT, E])
            for n in range(k):
                dst = mask if n == 0 else tmp
                chained(tr, DVE, DVE.tensor_tensor(dst[:, :, 0:E], io, bcast(topf[:, :, n], E), ALU.is_equal))
                yield
                if n:
                    chained(tr, DVE, DVE.tensor_tensor(mask[:, :, 0:E], mask[:, :, 0:E], tmp[:, :, 0:E], ALU.add))
                    yield

        def ffn0(updated, before_routing=lambda: None):
            E = 8
            CENTER, LOWER, UPPER = 1.0 / math.e, 0.5 - math.log(4.0 / 3.0), 0.5
            x_at, lg = routed_layernorm(Wr0, E, updated, a["ffn0_w"])
            before_routing()
            dv, ac = track("route_dve"), track("route_act")
            z, inh, w, fb = (r[n][:, :, 0:E] for n in "abcd")
            ps = bank[3][:, 0:NT * E].rearrange("p (t e) -> p t e", e=E)
            need(DVE, lg)
            c = lambda ins: chained(dv, DVE, ins)
            logits_read = dv.mark(DVE.tensor_scalar(z, ps, temp[:, 0:1], None, ALU.mult))
            need(SCL, logits_read)
            sigmoid_at = ac.mark(SCL.activation(z, z, ACT.Exp, scale=-1.0))

            def route():
                need(DVE, sigmoid_at)
                c(DVE.tensor_scalar(z, z, 1.0, None, ALU.add))
                yield
                c(DVE.reciprocal(inh, z))
                yield
                c(DVE.tensor_scalar(z, inh, CENTER, None, ALU.subtract))
                yield
                c(DVE.tensor_scalar(w, z, -1.0, None, ALU.mult))
                yield
                v = c(DVE.tensor_tensor(z, z, w, ALU.max))
                yield
                need(SCL, v)
                ac.mark(SCL.activation(w, z, ACT.Exp, scale=-10.0))
                v = ac.mark(SCL.activation(fb, z, ACT.Exp, scale=-1.0 / 0.3))
                need(DVE, v)
                c(DVE.tensor_scalar(z, inh, LOWER, None, ALU.is_ge))
                yield
                c(DVE.tensor_tensor(w, w, z, ALU.mult))
                yield
                c(DVE.tensor_scalar(z, inh, UPPER, None, ALU.is_le))
                yield
                c(DVE.tensor_tensor(w, w, z, ALU.mult))
                yield
                c(DVE.tensor_reduce(out=red["a"][:, :], in_=w, axis=AX, op=ALU.add))
                yield
                c(DVE.tensor_scalar(red["a"][:, :], red["a"][:, :], 1e-8, None, ALU.is_lt))
                yield
                c(DVE.tensor_scalar(red["b"][:, :], red["a"][:, :], -1.0, 1.0, ALU.mult, ALU.add))
                yield
                yield from top_mask(dv, r["d"], E, 2, r["a"], r["b"])
                c(DVE.tensor_tensor(fb, fb, z, ALU.mult))
                yield
                c(DVE.tensor_reduce(out=red["c"][:, :], in_=fb, axis=AX, op=ALU.add))
                yield
                c(DVE.tensor_scalar(red["c"][:, :], red["c"][:, :], 1e-8, None, ALU.max))
                yield
                c(DVE.reciprocal(red["c"][:, :], red["c"][:, :]))
                yield
                c(DVE.tensor_tensor(red["c"][:, :], red["c"][:, :], red["a"][:, :], ALU.mult))
                yield
                c(DVE.tensor_tensor(fb, fb, bcast(red["c"][:, :], E), ALU.mult))
                yield
                c(DVE.tensor_tensor(w, w, bcast(red["b"][:, :], E), ALU.mult))
                yield
                c(DVE.tensor_tensor(w, w, fb, ALU.add))
                yield
                c(DVE.tensor_reduce(out=red["c"][:, :], in_=w, axis=AX, op=ALU.add))
                yield
                c(DVE.tensor_scalar(red["c"][:, :], red["c"][:, :], 1e-8, None, ALU.max))
                yield
                c(DVE.reciprocal(red["c"][:, :], red["c"][:, :]))
                yield
                c(DVE.tensor_scalar(red["c"][:, :], red["c"][:, :], 0.5, None, ALU.mult))
                yield
                v = c(DVE.tensor_tensor(wtab[:, :, 0:E], w, bcast(red["c"][:, :], E), ALU.mult))
                yield

            return expert_loop(E, a["ffn0_w"], False, x_at, logits_read, route(), ROUTE0)

        def ffn1(updated):
            E = 32
            x_at, lg = routed_layernorm(Wr1, E, updated, a["ffn1_w"])
            dv, ac = track("route_dve"), track("route_act")
            z, w, sc = (r[n][:, :, :] for n in "abd")
            ps = bank[3][:, 0:NT * E].rearrange("p (t e) -> p t e", e=E)
            need(DVE, lg)
            c = lambda ins: chained(dv, DVE, ins)
            logits_read = c(DVE.tensor_tensor(z, ps, rbias[:, :].unsqueeze(1).broadcast_to([P, NT, E]), ALU.add))

            def route():
                c(DVE.tensor_reduce(out=red["a"][:, :], in_=z, axis=AX, op=ALU.max))
                yield
                v = c(DVE.tensor_tensor(z, z, bcast(red["a"][:, :], E), ALU.subtract))
                yield
                need(SCL, v)
                v = ac.mark(SCL.activation(z, z, ACT.Exp))
                need(DVE, v)
                c(DVE.tensor_reduce(out=red["a"][:, :], in_=z, axis=AX, op=ALU.add))
                yield
                c(DVE.reciprocal(red["a"][:, :], red["a"][:, :]))
                yield
                c(DVE.tensor_tensor(sc, z, bcast(red["a"][:, :], E), ALU.mult))
                yield
                yield from top_mask(dv, r["d"], E, 4, r["a"], r["b"])
                c(DVE.tensor_tensor(sc, sc, z, ALU.mult))
                yield
                c(DVE.tensor_reduce(out=red["a"][:, :], in_=sc, axis=AX, op=ALU.add))
                yield
                c(DVE.tensor_scalar(red["a"][:, :], red["a"][:, :], 1e-12, None, ALU.max))
                yield
                c(DVE.reciprocal(red["a"][:, :], red["a"][:, :]))
                yield
                c(DVE.tensor_scalar(red["a"][:, :], red["a"][:, :], 0.5, None, ALU.mult))
                yield
                c(DVE.tensor_tensor(wtab[:, :, 0:E], sc, bcast(red["a"][:, :], E), ALU.mult))
                yield

            return expert_loop(E, a["ffn1_w"], True, x_at, logits_read, route(), ROUTE1)

        H, HD, M = 16, 8, 64
        NK = H // 2
        R = S // M
        qT, kT = sb("qT", [P, T]), sb("kT", [P, T])
        v_sb = sb("v_sb", [P, NT, D])
        klm, qlm = sb("klm", [P, B, M]), sb("qlm", [P, B, M])
        QB, KB = sb("QB", [P, B, H * M]), sb("KB", [P, B, H * M])
        m1 = [sb(f"m1_{p}", [P, NK]) for p in range(2)]
        r1 = sb("r1", [P, NK, 2])
        E3, E3T = sg + [sb("E3_2", [P, GW])], hT
        m3, s3 = sb("m3", [P, B, NK]), sb("s3", [P, B, NK])
        m2, s2, rden = sb("m2", [P, NK]), sb("s2", [P, NK]), sb("rden", [P, B, NK])
        K = [sb(f"K{b}", [P, NK, M]) for b in range(B)]
        KT = sb("KT", [P, NK, M])
        E1 = [sb(f"E1_{p}", [P, H * M]) for p in range(2)]
        E1T = [sb(f"E1T_{p}", [P, NK, P]) for p in range(2)]
        TC = M + HD
        A, Q = ([sb(f"{n}{b}", [P, NK, TC]) for b in range(B)] for n in ("A", "Q"))
        y = [A[b][:, :, M:TC] for b in range(B)]
        A_part = [sb(f"A_part{b}", [P, NK, M]) for b in range(B)]
        y_part = [sb(f"y_part{b}", [P, NK, HD]) for b in range(B)]
        BD = E1T + [e[:, :].rearrange("p (k c) -> p k c", c=P) for e in E1]
        WC = 2 * HD + 2
        WB = sb("WB", [P, B, NK, WC])
        sv = [sb(f"sv{p}", [P, D]) for p in range(2)]
        svT = [sb(f"svT{p}", [P, D]) for p in range(2)]
        HALF = [slice(0, 64), slice(64, P)]
        pe, dv, ac, po = track("attn_pe"), track("attn_dve"), track("attn_act"), track("attn_pool")
        newton = [{n: track(f"newton{b}_{n}") for n in ("pe", "dve", "act")} for b in range(B)]

        def V(ins):
            return chained(dv, DVE, ins)

        def m8(ap2):
            return ap2.unsqueeze(2).broadcast_to([P, NK, M])

        def pv(b):
            return b[:, :].rearrange("p (k m) -> p k m", m=M)

        def attn0_constants():
            chained(po, POOL, POOL.memset(WB[:, :, :, :], 0.0))
            need(POOL, po.now())
            chained(po, POOL, POOL.memset(WB[0:64, :, :, 2 * HD:2 * HD + 1], 1.0))
            v = chained(po, POOL, POOL.memset(WB[64:P, :, :, 2 * HD + 1:WC], 1.0))
            for bd in BD:
                v = chained(po, POOL, POOL.memset(bd[:, :, :], 0.0))
            for e in (DVE, SCL, PE):
                need(e, v)

        def attn0(updated):
            xT = layernorm_T(updated)
            for e in (DVE, SCL, PE, POOL):
                need(e, updated[-1])
            q_at, k_at, v_at, QB_at, KB_at, klm_at, proj = ([None] * B for _ in range(7))
            free = {}

            def project(b):
                cols = slice(b * S, (b + 1) * S)
                bq, bk, bv = bank[3 * (b % 2)], bank[3 * (b % 2) + 1], bank[3 * (b % 2) + 2]
                need(PE, xT[b], *free.get(b - 2, ()))
                pq = pe.mark(PE.matmul(bq[:, :], wqkv[:, 0:D], xnT[:, cols], start=True, stop=True))
                pk = pe.mark(PE.matmul(bk[:, :], wqkv[:, D:2 * D], xnT[:, cols], start=True, stop=True))
                for j in range(TB):
                    t = b * TB + j
                    last = PE.matmul(bv[:, j * P:(j + 1) * P], xnT[:, t * P:(t + 1) * P], wqkv[:, 2 * D:3 * D],
                                     start=True, stop=True)
                pvv = pe.mark(last)
                need(SCL, pq)
                q_at[b] = ac.mark(SCL.mul(qT[:, cols], bq[:, :], HD ** -0.5))
                need(DVE, pk)
                k_at[b] = dv.mark(DVE.tensor_copy(kT[:, cols], bk[:, :]))
                need(SCL, pvv)
                v_at[b] = ac.mark(SCL.copy(v_sb[:, b * TB:(b + 1) * TB, :], bv[:, :].rearrange("p (j d) -> p j d", d=D)))
                free[b] = (q_at[b], k_at[b], v_at[b])

            def landmarks(b):
                cols = slice(b * S, (b + 1) * S)
                need(DVE, q_at[b], k_at[b])
                for src, lm in ((qT, qlm), (kT, klm)):
                    dv.mark(DVE.tensor_reduce(out=lm[:, b, :], in_=src[:, cols].rearrange("p (m r) -> p m r", r=R), axis=AX, op=ALU.add))
                need(DVE, dv.now())
                for lm in (qlm, klm):
                    klm_at[b] = dv.mark(DVE.tensor_scalar(lm[:, b, :], lm[:, b, :], 1.0 / R, None, ALU.mult))
                need(DVE, dv.now())
                need(POOL, dv.now())
                hm = headmask[:, :].unsqueeze(2).broadcast_to([P, H, M])
                for eng, tr, lm, dst, at in ((DVE, dv, qlm, QB, QB_at), (POOL, po, klm, KB, KB_at)):
                    at[b] = chained(tr, eng, eng.tensor_tensor(dst[:, b, :].rearrange("p (h m) -> p h m", m=M),
                                                      lm[:, b, :].unsqueeze(1).broadcast_to([P, H, M]), hm, ALU.mult))

            skew(B, project, landmarks)

            Qp = lambda b, k: QB[:, b, k * 2 * M:(k + 1) * 2 * M]
            y_at = {}
            e3_at, s_free, t_free, sc_at, tr_at, kv_done = {}, {}, {}, {}, {}, {}
            bankK, bank2 = (bank[4], bank[7]), bank[5]
            fronts = (q_at[-1], k_at[-1], v_at[-1])

            def scores3(i):
                b, k = divmod(i, NK)
                need(PE, QB_at[b], k_at[b], s_free.get(i - 2, fronts[0]), fronts[1], fronts[2])
                sc_at[i] = pe.mark(PE.matmul(bank[i % 2][:, :], Qp(b, k), kT[:, b * S:(b + 1) * S], start=True, stop=True))
                need(DVE, sc_at[i])
                v = dv.mark(DVE.tensor_reduce(out=m3[:, b, k:k + 1], in_=bank[i % 2][:, :], axis=AX, op=ALU.max, negate=True))
                need(SCL, v, tr_at.get(i - 3, (None, 0)))
                e3_at[i] = s_free[i] = ac.mark(SCL.activation(E3[i % 3][:, :], bank[i % 2][:, :], ACT.Exp,
                                                              bias=m3[:, b, k:k + 1], accum_out=s3[:, b, k:k + 1]))

            def transpose3(i):
                b, k = divmod(i, NK)
                bt = bank[2 + i % 2]
                need(PE, e3_at[i], t_free.get(i - 2, (None, 0)))
                for j in range(TB):
                    last = PE.transpose(bt[:, j * P:(j + 1) * P], E3[i % 3][:, j * P:(j + 1) * P], ident[:, :])
                tr_at[i] = pe.mark(last)
                eng, tr = ((SCL, ac), (DVE, dv))[i % 2]
                need(eng, tr_at[i], kv_done.get(i - 2, (None, 0)))
                cp = SCL.copy(E3T[i % 2][:, :], bt[:, :]) if eng is SCL else DVE.tensor_copy(E3T[i % 2][:, :], bt[:, :])
                t_free[i] = tr.mark(cp)

            def values3(i):
                b, k = divmod(i, NK)
                need(PE, t_free[i], y_at.get(b - 2, (None, 0)))
                for j in range(TB):
                    last = PE.matmul(bankK[b % 2][:, (b * NK + k) * 16:(b * NK + k + 1) * 16], E3T[i % 2][:, j * P:(j + 1) * P],
                                     v_sb[:, b * TB + j, k * 16:(k + 1) * 16], start=(j == 0), stop=(j == TB - 1))
                kv_done[i] = pe.mark(last)

            k2 = {}

            def kernel2(i):
                b, step = divmod(i, NK)
                kc = K[b]
                if step == 0:
                    need(PE, k2.get("A", fronts[2]), klm_at[b])
                    for k in range(NK):
                        last = PE.matmul(bank2[:, k * M:(k + 1) * M], Qp(b, k), klm[:, b, :], start=True, stop=True)
                    need(DVE, pe.mark(last))
                    V(DVE.tensor_reduce(out=m2[:, :], in_=pv(bank2), axis=AX, op=ALU.max))
                    k2["sub"] = dv.mark(DVE.tensor_tensor(kc[:, :, :], pv(bank2), m8(m2[:, :]), ALU.subtract))
                elif step == 1:
                    need(SCL, k2["sub"])
                    k2["exp"] = ac.mark(SCL.activation(kc[:, :, :], kc[:, :, :], ACT.Exp))
                elif step == 2:
                    need(DVE, k2["exp"])
                    V(DVE.tensor_reduce(out=s2[:, :], in_=kc[:, :, :], axis=AX, op=ALU.add))
                    V(DVE.reciprocal(s2[:, :], s2[:, :]))
                    k2["K"] = dv.mark(DVE.tensor_tensor(kc[:, :, :], kc[:, :, :], m8(s2[:, :]), ALU.mult))
                elif step == 4:
                    need(PE, k2["K"], k2["sub"], k2.get("KT", (None, 0)))
                    k2["sum"] = pe.mark(PE.matmul(bank2[:, :], blockones[:, :], kc[:, :, :], start=True, stop=True))
                    for k in range(NK):
                        for r in HALF:
                            last = PE.matmul(bank[6][r, k * M:(k + 1) * M], kc[r, k, :], ident2[r, :], start=True, stop=True)
                    k2["kt"] = pe.mark(last)
                    need(DVE, k2["sum"])
                    V(DVE.tensor_reduce(out=rden[:, b, :], in_=pv(bank2), axis=AX, op=ALU.max))
                    k2["rden"] = V(DVE.reciprocal(rden[:, b, :], rden[:, b, :]))
                    need(SCL, k2["kt"])
                    k2["KT"] = ac.mark(SCL.copy(KT[:, :, :], pv(bank[6])))
                elif step == 6:
                    need(PE, k2["KT"], k2["rden"])
                    for k in range(NK):
                        for r in HALF:
                            last = PE.matmul(bank2[r, k * M:(k + 1) * M], KT[r, k, :], KT[r, k, :], start=True, stop=True)
                    need(DVE, pe.mark(last))
                    k2["A"] = V(DVE.tensor_tensor(A[b][:, :, 0:M], pv(bank2), m8(rden[:, b, :]), ALU.mult))
                    need(POOL, k2["A"])
                    for h, r in enumerate(HALF):
                        k2["BD"] = po.mark(POOL.tensor_copy(BD[b][r, :, M * h:M * h + M], A[b][r, :, 0:M]))


            def normalise3(i):
                b, k = divmod(i, NK)
                if k != NK - 1:
                    return
                need(DVE, kv_done[i], e3_at[i])
                V(DVE.reciprocal(s3[:, b, :], s3[:, b, :]))
                kv = bankK[b % 2][:, :].rearrange("p (g d) -> p g d", d=2 * HD)
                for h, r in enumerate(HALF):
                    y_at[b] = dv.mark(DVE.tensor_tensor(A[b][r, :, M:TC], kv[r, b * NK:(b + 1) * NK, HD * h:HD * h + HD],
                                                        s3[r, b, :].unsqueeze(2).broadcast_to([64, NK, HD]), ALU.mult))

            skew(B * NK, scores3, kernel2, transpose3, values3, normalise3)

            need(SCL, y_at[B - 1], k2["BD"])
            need(DVE, y_at[B - 1])

            def mat(b, h):
                return bank[b + 4 * h][:, 0:4 * TC].rearrange("p (k c) -> p k c", c=TC)[:, :, 0:M]

            def vec(b, h):
                return bank[b + 4 * h][:, 0:4 * TC].rearrange("p (k c) -> p k c", c=TC)[:, :, M:TC]

            def square(b, X):
                for k in range(NK):
                    c = k % 4 * TC
                    last = PE.matmul(bank[b + 4 * (k // 4)][:, c:c + TC], BD[b][:, k, :], X[:, k, :], start=True, stop=True)
                return newton[b]["pe"].mark(last)

            def times_vectors(b, X):
                for k in range(NK):
                    for r in HALF:
                        c = k % 4 * TC
                        last = PE.matmul(bank[b + 4 * (k // 4)][r, c + M:c + TC], X[r, k, 0:M], X[r, k, M:TC],
                                         start=True, stop=True)
                return newton[b]["pe"].mark(last)

            def block_diagonal(b, X, at):
                need(SCL, at)
                for h, r in enumerate(HALF):
                    last = SCL.copy(BD[b][r, :, M * h:M * h + M], X[r, :, 0:M])
                newton[b]["act"].mark(last)

            def combine(out, in0, scalar, in1, op1):
                return DVE.scalar_tensor_tensor(out=out, in0=in0, scalar=scalar, in1=in1, op0=ALU.mult, op1=op1)

            def newton_step(first_step, last_step):
                for b in range(B):
                    need(PE, newton[b]["dve"].now(), newton[b]["act"].now())
                    if first_step:
                        need(PE, y_at[b], k2["BD"])
                    sq = square(b, A[b])
                    if not last_step:
                        need(SCL, newton[b]["dve"].now())
                        A_part_at = newton[b]["act"].mark(SCL.mul(A_part[b][:, :, :], A[b][:, :, 0:M], 13 / 4))
                    need(DVE, sq)
                    for h in range(2):
                        ks = slice(4 * h, 4 * h + 4)
                        last = combine(Q[b][:, ks, 0:M], A[b][:, ks, 0:M], -3.5, mat(b, h), ALU.add)
                    Q_at = newton[b]["dve"].mark(last)
                    if not last_step:
                        block_diagonal(b, Q[b], Q_at)
                        need(DVE, A_part_at)
                    for h in range(2):
                        ks = slice(4 * h, 4 * h + 4)
                        combine(Q[b][:, ks, M:TC], y[b][:, ks, :], 3.5, vec(b, h), ALU.subtract)
                        last = combine(y_part[b][:, ks, :], y[b][:, ks, :], 13 / 2.75, vec(b, h), ALU.subtract)
                        if not last_step:
                            last = combine(A_part[b][:, ks, :], mat(b, h), -2.75 / 4, A_part[b][:, ks, :], ALU.add)
                    newton[b]["dve"].mark(last)
                for b in range(B):
                    need(PE, newton[b]["dve"].now(), newton[b]["act"].now())
                    need(DVE, times_vectors(b, Q[b]) if last_step else square(b, Q[b]))
                    if not last_step:
                        for h in range(2):
                            ks = slice(4 * h, 4 * h + 4)
                            last = combine(A[b][:, ks, 0:M], mat(b, h), -0.25, A_part[b][:, ks, :], ALU.add)
                        block_diagonal(b, A[b], newton[b]["dve"].mark(last))
                    for h in range(2):
                        ks = slice(4 * h, 4 * h + 4)
                        last = combine(y[b][:, ks, :], y_part[b][:, ks, :], 2.75, vec(b, h), ALU.add)
                    need(DVE, newton[b]["dve"].mark(last))

            keep_busy(5, bank[0])
            for n in range(6):
                newton_step(n == 0, n == 5)

            for b in range(B):
                need(PE, newton[b]["dve"].now())
                for k in range(NK):
                    for r in HALF:
                        last = PE.matmul(bank[b][r, k * HD:(k + 1) * HD], K[b][r, k, :], A[b][r, k, M:TC], start=True, stop=True)
                need(DVE, pe.mark(last))
                for h, r in enumerate(HALF):
                    WB_at = dv.mark(DVE.scalar_tensor_tensor(
                        out=WB[r, b, :, HD * h:HD * h + HD], in0=bank[b][r, 0:NK * HD].rearrange("p (k d) -> p k d", d=HD),
                        scalar=0.25 ** 6, in1=rden[r, b, :].unsqueeze(2).broadcast_to([64, NK, HD]), op0=ALU.mult, op1=ALU.mult))
            need(PE, dv.now(), *(n["dve"].now() for n in newton))

            e1_at, h_free, c_done, t1_free, sv_done, sv_free, svT_done, svT_ev, pr_done = ({} for _ in range(9))

            def scores1(t):
                b, j = divmod(t, TB)
                need(PE, KB_at[b], q_at[b])
                for h in range(2):
                    i = 2 * t + h
                    need(PE, h_free.get(i - 3, (None, 0)))
                    at = pe.mark(PE.matmul(bank[i % 3][:, :], qT[:, t * P:(t + 1) * P], KB[:, b, h * 512:(h + 1) * 512], start=True, stop=True))
                    need(DVE, at, c_done.get(t - 2, (None, 0)))
                    V(DVE.tensor_reduce(out=m1[h][:, :], in_=pv(bank[i % 3]), axis=AX, op=ALU.max))
                    h_free[i] = dv.mark(DVE.tensor_tensor(E1[t % 2][:, h * 512:(h + 1) * 512].rearrange("p (k m) -> p k m", m=M),
                                                          pv(bank[i % 3]), m8(m1[h][:, :]), ALU.subtract))
                    need(SCL, h_free[i])
                    e1_at[t] = ac.mark(SCL.activation(E1[t % 2][:, h * 512:(h + 1) * 512], E1[t % 2][:, h * 512:(h + 1) * 512], ACT.Exp))

            def transpose1(t):
                need(PE, e1_at[t])
                for h in range(2):
                    need(PE, t1_free.get((t - 1, h), (None, 0)))
                    for k in range(4):
                        last = PE.transpose(bank[3 + h][:, k * P:(k + 1) * P], E1[t % 2][:, (4 * h + k) * P:(4 * h + k + 1) * P], ident[:, :])
                    c_done[t] = pe.mark(last)
                    need(SCL, c_done[t], sv_done.get(t - 2, (None, 0)))
                    t1_free[t, h] = ac.mark(SCL.copy(E1T[t % 2][:, 4 * h:4 * h + 4, :], bank[3 + h][:, :].rearrange("p (k t) -> p k t", t=P)))

            def values1(t):
                b = t // TB
                need(PE, t1_free[t, 1], sv_free.get(t - 1, (None, 0)))
                for k in range(NK):
                    last = PE.matmul(bank[5][:, k * WC:(k + 1) * WC], E1T[t % 2][:, k, :], WB[:, b, k, :], start=True, stop=True)
                sv_done[t] = pe.mark(last)
                o = bank[5][:, 0:NK * WC].rearrange("p (k c) -> p k c", c=WC)
                need(DVE, sv_done[t], svT_done.get(t - 2, (None, 0)))
                V(DVE.reciprocal(r1[:, :, :], o[:, :, 2 * HD:WC]))
                sv_free[t] = dv.mark(DVE.tensor_tensor(sv[t % 2][:, :].rearrange("p (k h d) -> p k h d", h=2, d=HD),
                                                       o[:, :, 0:2 * HD].rearrange("p k (h d) -> p k h d", d=HD),
                                                       r1[:, :, :].unsqueeze(3).broadcast_to([P, NK, 2, HD]), ALU.mult))

            def transpose_sv(t):
                need(PE, sv_free[t], svT_ev.get(t - 1, (None, 0)))
                svT_done[t] = pe.mark(PE.transpose(bank[6][:, 0:P], sv[t % 2][:, :], ident[:, :]))
                need(SCL, svT_done[t], pr_done.get(t - 2, (None, 0)))
                svT_ev[t] = ac.mark(SCL.copy(svT[t % 2][:, :], bank[6][:, 0:P]))

            res = {}

            def output(t):
                need(PE, svT_ev[t], res.get(t - 1, (None, 0)))
                pr_done[t] = pe.mark(PE.matmul(bank[7][:, 0:D], svT[t % 2][:, :], wproj[:, :], start=True, stop=True))
                need(DVE, pr_done[t])
                res[t] = s_res.mark(DVE.tensor_tensor(x[:, t, :], bank[7][:, 0:D], x[:, t, :], ALU.add))

            skew(NT, scores1, transpose1, values1, transpose_sv, output)
            return [res[TB * b + TB - 1] for b in range(B)]

        NW = 2 * S // P - 1
        Ew = [sb(f"Ew{p}", [P, P]) for p in range(3)]
        EwT = [sb(f"EwT{p}", [P, P]) for p in range(2)]
        mw, sw = sb("mw", [P, B * NW]), sb("sw", [P, B * NW])
        bqs = sb("bqs", [P, 1])
        oT = [sb(f"oT{p}", [P, S]) for p in range(2)]
        ORDER = [w for w in range(0, NW, 2)] + [w for w in range(1, NW, 2)]

        def attn1(updated):
            SC = 1.0 / math.sqrt(8.0)
            xT = layernorm_T(updated)
            for e in (DVE, SCL, PE, POOL):
                need(e, updated[-1])
            vw = QB
            V(DVE.tensor_scalar(bqs[:, :], bq1[:, :], SC, None, ALU.mult))
            need(SCL, dv.now())
            q_at, k_at, v_at = ([None] * B for _ in range(3))

            def project(b):
                cols = slice(b * S, (b + 1) * S)
                need(PE, xT[b])
                if b:
                    need(PE, q_at[b - 1], k_at[b - 1])
                pq = pe.mark(PE.matmul(bank[0][:, :], wq1[:, :], xnT[:, cols], start=True, stop=True))
                pk = pe.mark(PE.matmul(bank[1][:, :], wk1[:, :], xnT[:, cols], start=True, stop=True))
                need(SCL, pq)
                q_at[b] = ac.mark(SCL.activation(qT[:, cols], bank[0][:, :], ACT.Identity, bias=bqs[:, 0:1], scale=SC))
                need(SCL, pk)
                k_at[b] = ac.mark(SCL.activation(kT[:, cols], bank[1][:, :], ACT.Identity, bias=bk1[:, 0:1]))
                for g, n in ((0, 4), (1, NW - 4)):
                    bk = bank[2 + 2 * (b % 2) + g]
                    if b > 1:
                        need(PE, v_at[b - 2])
                    for w in range(n):
                        c = b * S + (4 * g + w) * 64
                        last = PE.matmul(bk[:, w * P:(w + 1) * P], xnT[:, c:c + P], wv1[:, :], start=True, stop=True)
                    need(DVE, pe.mark(last))
                    v_at[b] = dv.mark(DVE.tensor_tensor(vw[:, b, 4 * g * D:(4 * g + n) * D].rearrange("p (w d) -> p w d", d=D),
                                                        bk[:, 0:n * P].rearrange("p (w d) -> p w d", d=D),
                                                        bv1[:, :].unsqueeze(1).broadcast_to([P, n, D]), ALU.add))

            for b in range(B):
                project(b)
            need(PE, dv.now(), ac.now())
            s_at, n_at, t_at, c_at, o_at, res = ({} for _ in range(6))

            def scores(i):
                b, n = divmod(i, NW)
                w = ORDER[n]
                win = slice(b * S + w * 64, b * S + w * 64 + P)
                bs, e = bank[i % 2], Ew[i % 3]
                need(PE, s_at.get(i - 2, (None, 0)))
                need(DVE, pe.mark(PE.matmul(bs[:, 0:P], qT[:, win], kT[:, win], start=True, stop=True)))
                v = dv.mark(DVE.tensor_reduce(out=mw[:, i:i + 1], in_=bs[:, 0:P], axis=AX, op=ALU.max, negate=True))
                need(SCL, v, t_at.get(i - 3, (None, 0)))
                s_at[i] = ac.mark(SCL.activation(e[:, :], bs[:, 0:P], ACT.Exp, bias=mw[:, i:i + 1], accum_out=sw[:, i:i + 1]))

            def normalise(i):
                e = Ew[i % 3]
                need(DVE, s_at[i])
                V(DVE.reciprocal(sw[:, i:i + 1], sw[:, i:i + 1]))
                n_at[i] = dv.mark(DVE.tensor_scalar(e[:, :], e[:, :], sw[:, i:i + 1], None, ALU.mult))

            def transposed(i):
                need(PE, n_at[i], c_at.get(i - 2, (None, 0)))
                t_at[i] = pe.mark(PE.transpose(bank[2 + i % 2][:, 0:P], Ew[i % 3][:, :], ident[:, :]))
                need(SCL, t_at[i], o_at.get(i - 2, (None, 0)))
                c_at[i] = ac.mark(SCL.copy(EwT[i % 2][:, :], bank[2 + i % 2][:, 0:P]))

            ev = {}

            def values(i):
                b, n = divmod(i, NW)
                w = ORDER[n]
                bo = bank[4 + b % 2]
                need(PE, c_at[i], ev.get(b - 2, (None, 0)))
                o_at[i] = pe.mark(PE.matmul(bo[:, w * 64:w * 64 + P], vw[:, b, w * D:(w + 1) * D], EwT[i % 2][:, :],
                                            start=(n == 0), stop=(n == NW - 1), skip_group_check=True))
                if n == NW - 1:
                    need(SCL, o_at[i], res.get(b - 2, (None, 0)))
                    o = oT[b % 2]
                    SCL.copy(o[:, 0:64], bo[:, 0:64])
                    SCL.mul(o[:, 64:S - 64], bo[:, 64:S - 64], 0.5)
                    ev[b] = ac.mark(SCL.copy(o[:, S - 64:S], bo[:, S - 64:S]))

            def output(i):
                b, n = divmod(i, NW)
                if n != NW - 1:
                    return
                bo = bank[6 + b % 2]
                need(PE, ev[b], res.get(b - 2, (None, 0)))
                for j in range(TB):
                    last = PE.matmul(bo[:, j * P:(j + 1) * P], oT[b % 2][:, j * P:(j + 1) * P], wo1[:, :], start=True, stop=True)
                need(DVE, pe.mark(last))
                xs = x[:, b * TB:(b + 1) * TB, :]
                V(DVE.tensor_tensor(xs, bo[:, :].rearrange("p (j d) -> p j d", d=D), xs, ALU.add))
                res[b] = s_res.mark(DVE.tensor_tensor(xs, xs, bo1[:, :].unsqueeze(1).broadcast_to([P, TB, D]), ALU.add))

            skew(B * NW, scores, normalise, transposed, values, output)
            return [res[b] for b in range(B)]

        up = ffn0(loaded_x, small_operands)
        attn0_constants()
        up = attn0(up)
        up = ffn0(up)
        up = ffn1(up)
        up = attn1(up)
        up = ffn1(up)
        s_out = track("stored", 16)
        need(SP, s_res.now())
        s_out.mark(SP.dma_start(out.rearrange("b (t p) d -> p (b t) d", p=P), x[:, :, :]))
        need(SP, s_out.now())


LOOP_TRACKS = ("expert_load0 expert_load1 expert_gate expert_up expert_down expert_split0 expert_split1 expert_silu expert_hidden "
               "x_updated").split()

_X = "x wqkv wproj Wr temp WrT rbias Wq Wk Wv Wo bq bk bv bo ffn0_w ffn1_w".split()


def kernel(**inputs):
    import numpy as _np
    import concourse.bacc as _bacc
    from concourse import mybir as _mybir
    from concourse.bass_utils import run_bass_kernel_spmd as _run

    i = {k: _np.asarray(v) for k, v in inputs.items()}
    t = lambda w: w.transpose(0, 2, 1)
    rows = lambda w: w.reshape(4, P, w.shape[1])
    g0, u0, d0 = (i[f"L0_ffn_{n}"] for n in ("Wg", "Wu", "Wd"))
    g1 = _np.concatenate([t(rows(i["L1_ffn_sgate_w"])), t(i["L1_ffn_gate_w"])])
    u1 = _np.concatenate([t(rows(i["L1_ffn_sup_w"])), t(i["L1_ffn_up_w"])])
    d1 = _np.concatenate([i["L1_ffn_sdown_w"].T.reshape(4, P, P), t(i["L1_ffn_down_w"])])
    a = {
        "x": i["L0_attn_x"], "wqkv": i["L0_attn_w_qkv"], "wproj": i["L0_attn_w_proj"],
        "Wr": i["L0_ffn_Wr"], "temp": i["L0_ffn_temperature"],
        "WrT": i["L1_ffn_router_w"].T, "rbias": i["L1_ffn_router_bias"],
        "Wq": i["L1_attn_Wq"], "Wk": i["L1_attn_Wk"], "Wv": i["L1_attn_Wv"], "Wo": i["L1_attn_Wo"],
        "bq": i["L1_attn_bq"], "bk": i["L1_attn_bk"], "bv": i["L1_attn_bv"], "bo": i["L1_attn_bo"],
        "ffn0_w": _np.stack([g0, u0, d0], axis=2),
        "ffn1_w": _np.stack([g1, u1, d1], axis=2),
    }
    nc = _bacc.Bacc("TRN2", target_bir_lowering=False, num_devices=1)
    arrays, aps = {}, {}
    for name in _X:
        v = _np.ascontiguousarray(a[name])
        arrays[f"in_{name}"] = v
        aps[name] = nc.dram_tensor(f"in_{name}", v.shape, _mybir.dt.from_np(v.dtype), kind="ExternalInput").ap()
    out = nc.dram_tensor("out", a["x"].shape, _mybir.dt.float32, kind="ExternalOutput").ap()
    build(nc, aps, out)
    return _run(nc, [arrays], core_ids=[0]).results[0]["out"]
```
